# Optimizing a Trainium2 kernel written in Bass

```python
import numpy as np
import jax
import jax.numpy as jnp

def _softmax(x, axis=-1):
    return jax.nn.softmax(x, axis=axis)

def _gelu(x):
    return jax.nn.gelu(x, approximate=True)

def _silu(x):
    return jax.nn.silu(x)

def _sigmoid(x):
    return jax.nn.sigmoid(x)

def _layernorm(x, axis=-1, eps=1e-05):
    m = jnp.mean(x, axis=axis, keepdims=True)
    v = jnp.var(x, axis=axis, keepdims=True)
    return (x - m) / jnp.sqrt(v + eps)

def _scatter_add(tgt, idx, src, axis=0):
    return tgt.at[idx].add(src)

def _segment_sum(src, seg, n):
    return jax.ops.segment_sum(src, seg, n)
kernel_name = 'mk_gnn_preln_d1_gnn_r64_5ff5a5'

def setup_inputs(seed: int=0):
    np.random.seed(seed)
    _w = jnp.asarray

    def _rec_inputs():
        import jax
        import jax.numpy as jnp
        _gk = jax.random.key(seed)
        x = -0.0005121 + 1.001 * jax.random.normal(jax.random.fold_in(_gk, 1), (100000, 64), jnp.float32)
        src = jax.random.randint(jax.random.fold_in(_gk, 2), (25000,), 0, 100000, jnp.int32)
        dst = jax.random.randint(jax.random.fold_in(_gk, 3), (25000,), 0, 100000, jnp.int32)
        _o = jnp.argsort(dst, stable=True)
        src = src[_o]
        dst = dst[_o]
        edge_attr_64 = -9.77346e-05 + 0.999888 * jax.random.normal(jax.random.fold_in(_gk, 11), (25000, 64), jnp.float32)
        return (x, src, dst, edge_attr_64)
    x, src, dst, edge_attr_64 = _rec_inputs()

    def _L0_gnn_setup():
        import jax, jax.numpy as jnp
        import numpy as np
        N_ATOMS = 50000
        N_EDGES = 12500
        NODE_DIM = 64
        EDGE_DIM = 64
        FULL_DIM = 2 * NODE_DIM + EDGE_DIM
        BN_EPS = 1e-05

        def _batchnorm(x, gamma, beta):
            mean = jnp.mean(x, axis=0)
            var = jnp.mean(jnp.square(x - mean), axis=0)
            return (x - mean) * jax.lax.rsqrt(var + BN_EPS) * gamma + beta
        key = jax.random.key(seed)
        ks = jax.random.split(key, 8)
        atom_features = jax.random.normal(ks[0], (N_ATOMS, NODE_DIM), dtype=jnp.float32)
        edge_features = jax.random.normal(ks[1], (N_EDGES, EDGE_DIM), dtype=jnp.float32)
        edge_indices = jax.random.randint(ks[2], (N_EDGES, 2), 0, N_ATOMS, dtype=jnp.int64)
        lim = 1.0 / np.sqrt(FULL_DIM)
        W_filter = jax.random.uniform(ks[3], (NODE_DIM, FULL_DIM), jnp.float32, -lim, lim)
        b_filter = jax.random.uniform(ks[4], (NODE_DIM,), jnp.float32, -lim, lim)
        W_core = jax.random.uniform(ks[5], (NODE_DIM, FULL_DIM), jnp.float32, -lim, lim)
        b_core = jax.random.uniform(ks[6], (NODE_DIM,), jnp.float32, -lim, lim)
        gamma_filter = jnp.ones((NODE_DIM,), jnp.float32)
        beta_filter = jnp.zeros((NODE_DIM,), jnp.float32)
        gamma_core = jnp.ones((NODE_DIM,), jnp.float32)
        beta_core = jnp.zeros((NODE_DIM,), jnp.float32)
        return {'atom_features': atom_features, 'edge_features': edge_features, 'W_filter': W_filter, 'b_filter': b_filter, 'gamma_filter': gamma_filter, 'beta_filter': beta_filter, 'W_core': W_core, 'b_core': b_core, 'gamma_core': gamma_core, 'beta_core': beta_core, 'edge_indices': edge_indices}
    _L0_gnn_all = _L0_gnn_setup()
    _L0_gnn_in = {k: v for k, v in _L0_gnn_all.items() if k in ('W_filter', 'b_filter', 'gamma_filter', 'beta_filter', 'W_core', 'b_core', 'gamma_core', 'beta_core')}
    del _L0_gnn_all
    return {'x': x, 'src': src, 'dst': dst, 'edge_attr_64': edge_attr_64, 'L0_gnn_W_filter': _L0_gnn_in['W_filter'], 'L0_gnn_b_filter': _L0_gnn_in['b_filter'], 'L0_gnn_gamma_filter': _L0_gnn_in['gamma_filter'], 'L0_gnn_beta_filter': _L0_gnn_in['beta_filter'], 'L0_gnn_W_core': _L0_gnn_in['W_core'], 'L0_gnn_b_core': _L0_gnn_in['b_core'], 'L0_gnn_gamma_core': _L0_gnn_in['gamma_core'], 'L0_gnn_beta_core': _L0_gnn_in['beta_core']}

def reference(x, src, dst, edge_attr_64, L0_gnn_W_filter, L0_gnn_b_filter, L0_gnn_gamma_filter, L0_gnn_beta_filter, L0_gnn_W_core, L0_gnn_b_core, L0_gnn_gamma_core, L0_gnn_beta_core):
    import jax
    import jax.numpy as jnp

    def _L0_gnn_ref(atom_features, edge_features, W_filter, b_filter, gamma_filter, beta_filter, W_core, b_core, gamma_core, beta_core, edge_indices):
        import jax, jax.numpy as jnp
        import numpy as np
        N_ATOMS = 50000
        N_EDGES = 12500
        NODE_DIM = 64
        EDGE_DIM = 64
        FULL_DIM = 2 * NODE_DIM + EDGE_DIM
        BN_EPS = 1e-05

        def _batchnorm(x, gamma, beta):
            mean = jnp.mean(x, axis=0)
            var = jnp.mean(jnp.square(x - mean), axis=0)
            return (x - mean) * jax.lax.rsqrt(var + BN_EPS) * gamma + beta
        src = edge_indices[:, 0]
        dst = edge_indices[:, 1]
        z = jnp.concatenate([atom_features[dst], atom_features[src], edge_features], axis=1)
        signal = jax.nn.softplus(_batchnorm(z @ W_core.T + b_core, gamma_core, beta_core))
        gate = jax.nn.sigmoid(_batchnorm(z @ W_filter.T + b_filter, gamma_filter, beta_filter))
        message = gate * signal
        nbr_sumed = jax.ops.segment_sum(message, dst, num_segments=atom_features.shape[0])
        return atom_features + nbr_sumed
    edge_index_t = jnp.stack([src, dst], axis=1)
    h = jnp.maximum(_layernorm(x, axis=-1), 0.0)
    x = x + _L0_gnn_ref(h, edge_attr_64, L0_gnn_W_filter, L0_gnn_b_filter, L0_gnn_gamma_filter, L0_gnn_beta_filter, L0_gnn_W_core, L0_gnn_b_core, L0_gnn_gamma_core, L0_gnn_beta_core, edge_index_t)
    return x

_drawn_inputs = setup_inputs


def setup_inputs(seed=0):
    import zlib

    import numpy as np

    out = dict(_drawn_inputs(seed))
    spreads = {'L0_gnn_gamma_filter': (1.0, 0.6),
     'L0_gnn_beta_filter': (0.0, 0.8),
     'L0_gnn_gamma_core': (1.0, 0.6),
     'L0_gnn_beta_core': (0.0, 0.768)}
    factors = {'L0_gnn_b_filter': 8.0, 'L0_gnn_b_core': 8.0}
    for name, (base, spread) in spreads.items():
        noise = np.random.default_rng([zlib.crc32(name.encode()), seed]).standard_normal(out[name].shape)
        drawn = base * np.exp(spread * noise) if base else spread * noise
        out[name] = jnp.asarray(drawn.astype(out[name].dtype))
    for name, factor in factors.items():
        out[name] = (out[name] * factor).astype(out[name].dtype)
    return out
```

```python
from contextlib import ExitStack

import concourse.bass as bass
from concourse import mybir

F32 = mybir.dt.float32
I32 = mybir.dt.int32
ALU = mybir.AluOpType
ACT = mybir.ActivationFunctionType
AX_X = mybir.AxisListType.X
P = 128
RING = 4
BIG = float(1 << 20)
LN_EPS = 1e-5
BN_EPS = 1e-5


class Turn:

    def __init__(self, eng, i, j, shift=0, known=None):
        self.eng, self.i, self.j, self.shift, self.known = eng, i, j, shift, {} if known is None else known
        if isinstance(i, int):
            self.i, self.shift = i + shift, 0

    def back(self, n):
        at = self.j - n
        return Turn(self.eng, self.i, at % RING, self.shift + at // RING, self.known)

    def exists(self):
        return not isinstance(self.i, int) or self.i >= 0

    def is_number(self, k):
        return isinstance(self.i, int) and RING * self.i + self.j == k

    def linear(self, scale, add):
        if isinstance(self.i, int):
            return scale * self.i + add
        if (scale, add) not in self.known:
            self.known[scale, add] = self.eng.snap(self.i * scale + add)
        return self.known[scale, add]

    def count(self, unit):
        return self.linear(unit, unit * (self.shift + 1))

    def count_all(self, unit, short=0):
        return self.linear(unit * RING, unit * (RING * self.shift + self.j + 1) - short)

    def at(self, step):
        return self.linear(step * RING, step * (RING * self.shift + self.j))


def wait_turn(eng, semaphore, turn, unit=1, short=0):
    if turn.exists():
        eng.wait_ge(semaphore, turn.count_all(unit, short))


def wait_slot(eng, semaphores, turn, count):
    if turn.exists():
        eng.wait_ge(semaphores[turn.j], turn.count(16 * count))


def run_turns(eng, turns, body):
    for j in range(RING):
        body(Turn(eng, 0, j))
    with eng.Fori(1, turns // RING) as i:
        known = {}
        for j in range(RING):
            body(Turn(eng, i, j, known=known))
    for k in range(turns // RING * RING, turns):
        body(Turn(eng, k // RING, k % RING))


def gnn_layer(nc, x, src, dst, edge_attr, w_filter, b_filter, g_filter, be_filter,
              w_core, b_core, g_core, be_core, out):
    N, D = x.shape
    E = edge_attr.shape[0]
    G = 4
    C = 2 * D
    EDGE_COLS = -(-E // P)
    TURNS = EDGE_COLS // G
    DUP = P * EDGE_COLS - E
    NODE_ROWS = N // P
    REST = N - P * NODE_ROWS
    R = -(-NODE_ROWS // TURNS)
    R_LAST = NODE_ROWS - R * (TURNS - 1)
    ROWS = R + 2 * G
    assert D == 64 and C == P and EDGE_COLS % G == 0 and TURNS % RING == 1 and DUP < EDGE_COLS
    assert 0 < R_LAST <= R and 0 < REST <= P
    PA = (P - 1) // 16 * 16
    CHUNKS = TURNS + 1

    x_rows = x[0:P * NODE_ROWS, :].rearrange("(p r) d -> p r d", p=P)
    out_rows = out[0:P * NODE_ROWS, :].rearrange("(p r) d -> p r d", p=P)
    edge_rows = edge_attr[0:(P - 1) * EDGE_COLS, :].rearrange("(p t) d -> p t d", p=P - 1)
    edge_last = edge_attr[E - EDGE_COLS:E, :].rearrange("(p t) d -> p t d", p=1)

    ctx = ExitStack()
    with ctx:
        def sb(name, shape, dt=F32):
            return ctx.enter_context(nc.sbuf_tensor(name, shape, dt))

        def sem(name):
            return ctx.enter_context(nc.semaphore(name))

        def sems(name):
            return [sem(f"{name}{j}") for j in range(RING)]

        ident = sb("ident", [P, P])
        lower = sb("lower", [P, P])
        ones = sb("ones", [P, P])
        w_cat = sb("w_cat", [P, 2 * D])
        w_edge = sb("w_edge", [P, D])
        wt_nodes = sb("wt_nodes", [P, C])
        wt_edge = sb("wt_edge", [D, C])
        bias = sb("bias", [P, 1])
        gamma = sb("gamma", [P, 1])
        beta = sb("beta", [P, 1])
        ln_eps = sb("ln_eps", [P, 1])
        idx = sb("idx", [P, 2, EDGE_COLS + RING * G], I32)
        gather_idx = sb("gather_idx", [P, RING, 2, G], I32)
        dst_once = sb("dst_once", [P, EDGE_COLS], I32)
        dst_next = sb("dst_next", [P, EDGE_COLS], I32)
        same = sb("same", [P, EDGE_COLS])
        falls = sb("falls", [P, EDGE_COLS])
        dst_f = sb("dst_f", [P, EDGE_COLS])
        goes_now = sb("goes_now", [P, RING, G])
        run_idx = sb("run_idx", [P, EDGE_COLS], I32)
        goes_on = sb("goes_on", [P, EDGE_COLS])
        nfalls = sb("nfalls", [P, 1])
        is_sorted = sb("is_sorted", [P, 1])
        unsorted = sb("unsorted", [P, 1], I32)
        pre = sb("pre", [P, TURNS * G * P])
        xin = sb("xin", [P, RING, ROWS, D])
        xc = sb("xc", [P, 2, ROWS, D])
        sq = sb("sq", [P, ROWS, D])
        xsum = sb("xsum", [P, 2, ROWS])
        var = sb("var", [P, 2, ROWS])
        std = sb("std", [P, 2, ROWS])
        rstd = sb("rstd", [P, 2, ROWS])
        h = sb("h", [P, 2, ROWS, D])
        y = sb("y", [P, 2, R, D])
        edge = sb("edge", [P, RING, G, D])
        zt = sb("zt", [P, 2, G * P])
        et = sb("et", [D, 2, G * P])
        stats = sb("stats", [P, CHUNKS, 6])
        rest = sb("rest", [P, 6, D])
        rest_c = sb("rest_c", [P, 8])
        moments = sb("moments", [P, 2])
        bn = sb("bn", [P, 6])
        an = zt
        spare = h[:].rearrange("p a r d -> p (a r) d")
        e_gate, c_abs, e_core, log1p = (
            spare[:, n * 2 * G:(n + 1) * 2 * G, :].rearrange("p (b g) d -> p b g d", b=2) for n in range(4))
        den = sb("den", [P, G, D])
        gate = sb("gate", [P, G, D])
        signal = sb("signal", [P, G, D])
        msg = sb("msg", [P, G, D])
        run = sb("run", [P, RING, G, D])
        scatter_idx = sb("scatter_idx", [P, RING, G], I32)
        key = sb("key", [P, 1])
        keys = sb("keys", [P, P])
        equal = sb("equal", [P, P])
        earlier = sb("earlier", [P, P])
        repeats = sb("repeats", [P, 2])
        once_idx = sb("once_idx", [P, 1], I32)
        part = sb("part", [P, D])
        total = sb("total", [P, D])

        def banks(name, shape):
            return [ctx.enter_context(nc.psum_tensor(f"{name}{b}", shape, F32)) for b in range(2)]

        zt_ps = banks("zt_ps", [P, G * P])
        et_ps = banks("et_ps", [P, G * P])
        pre_ps = banks("pre_ps", [P, G * P])
        w_ps = ctx.enter_context(nc.psum_tensor("w_ps", [P, 512], F32))
        k_ps = ctx.enter_context(nc.psum_tensor("k_ps", [P, 512], F32))

        idx_loaded = sem("idx_loaded")
        const_loaded = sem("const_loaded")
        const_made = sem("const_made")
        waited = sem("waited")
        pads_set = sem("pads_set")
        w_turned = sem("w_turned")
        w_ready = sem("w_ready")
        rest_loaded = sem("rest_loaded")
        rest_stored = sem("rest_stored")
        rest_var = sem("rest_var")
        rest_ready = sem("rest_ready")
        rest_std = sem("rest_std")
        link = sem("link")
        bn_ready = sem("bn_ready")
        falls_ready = sem("falls_ready")
        falls_summed = sem("falls_summed")
        runs_ready = sem("runs_ready")
        idx_staged = sem("idx_staged")
        gathered = sems("gathered")
        nodes_loaded = sems("nodes_loaded")
        edges_loaded = sems("edges_loaded")
        summed = sem("summed")
        centred = sem("centred")
        squared = sem("squared")
        var_ready = sem("var_ready")
        std_ready = sem("std_ready")
        rstd_ready = sem("rstd_ready")
        h_ready = sem("h_ready")
        y_ready = sem("y_ready")
        y_stored = sems("y_stored")
        rows_turned = sem("rows_turned")
        zt_copied = sem("zt_copied")
        et_copied = sem("et_copied")
        multiplied = sem("multiplied")
        pre_copied = sem("pre_copied")
        counted = sem("counted")
        bn_var = sem("bn_var")
        bn_std = sem("bn_std")
        affine_done = sem("affine_done")
        act_turned = sem("act_turned")
        gate_exp = sem("gate_exp")
        abs_done = sem("abs_done")
        core_exp = sem("core_exp")
        log_done = sem("log_done")
        one_added = sem("one_added")
        gate_ready = sem("gate_ready")
        signal_ready = sem("signal_ready")
        msg_ready = sem("msg_ready")
        run_step = sem("run_step")
        sidx_staged = sem("sidx_staged")
        goes_staged = sem("goes_staged")
        scattered = sems("scattered")
        run_kept = sem("run_kept")
        def combine_sems(name):
            return {s: sem(f"{name}_{s}") for s in
                    ("key", "keys", "turned", "equal", "earlier", "counted", "flagged", "idx", "part", "summed",
                     "total", "added")}
        tail = combine_sems("tail")
        each = combine_sems("each")

        block = ctx.enter_context(nc.Block())

        @block.sync
        def _(sp):
            sp.wait_ge(pads_set, 3)
            for k, table in enumerate((dst, src)):
                rows = table[0:(P - 1) * EDGE_COLS].rearrange("(p t) -> p t", p=P - 1)
                sp.dma_start(idx[0:PA, k, 0:EDGE_COLS], rows[0:PA, :]).then_inc(idx_loaded, 16)
                sp.dma_start(idx[PA:P - 1, k, 0:EDGE_COLS], rows[PA:P - 1, :]).then_inc(idx_loaded, 16)
                sp.dma_start(idx[P - 1:P, k, 0:EDGE_COLS],
                             table[E - EDGE_COLS:E].rearrange("(p t) -> p t", p=1)).then_inc(idx_loaded, 16)

            def loads(t, rows):
                wait_turn(sp, y_ready, t.back(RING))
                sp.dma_start(xin[:, t.j, 0:rows, :], x_rows[:, bass.ds(t.at(R), rows), :]).then_inc(
                    nodes_loaded[t.j], 16)
                wait_turn(sp, rows_turned, t.back(RING))
                for d, s in ((edge[0:PA], edge_rows[0:PA]), (edge[PA:P - 1], edge_rows[PA:P - 1]),
                             (edge[P - 1:P], edge_last)):
                    sp.dma_start(d[:, t.j, :, :], s[:, bass.ds(t.at(G), G), :]).then_inc(edges_loaded[t.j], 16)

            def store(t, rows):
                wait_turn(sp, y_ready, t)
                sp.dma_start(out_rows[:, bass.ds(t.at(R), rows), :], y[:, t.j % 2, 0:rows, :]).then_inc(
                    y_stored[t.j], 16)

            def turn(t):
                if t.back(RING).exists():
                    store(t.back(RING), R)
                loads(t, R_LAST if t.is_number(TURNS - 1) else R)
                if t.is_number(1):
                    small_loads()

            def small_loads():
                sp.dma_start(rest[0:REST, 0, :], x[P * NODE_ROWS:N, :]).then_inc(rest_loaded, 16)
                for w, at in ((w_filter, 0), (w_core, D)):
                    sp.dma_start(w_cat[at:at + D, :], w[:, 0:2 * D]).then_inc(const_loaded, 16)
                    sp.dma_start(w_edge[at:at + D, :], w[:, 2 * D:3 * D]).then_inc(const_loaded, 16)
                for col, filt, core in ((bias, b_filter, b_core), (gamma, g_filter, g_core),
                                        (beta, be_filter, be_core)):
                    for v, at in ((filt, 0), (core, D)):
                        sp.dma_start(col[at:at + D, :], v.rearrange("(d o) -> d o", o=1)).then_inc(const_loaded, 16)
                rows = dst[0:(P - 1) * EDGE_COLS].rearrange("(p t) -> p t", p=P - 1)
                after = dst[1:(P - 1) * EDGE_COLS + 1].rearrange("(p t) -> p t", p=P - 1)
                for d, s in ((dst_once, rows), (dst_next, after)):
                    sp.dma_start(d[0:PA, :], s[0:PA, :]).then_inc(const_loaded, 16)
                    sp.dma_start(d[PA:P - 1, :], s[PA:P - 1, :]).then_inc(const_loaded, 16)
                sp.dma_start(dst_once[P - 1:P, DUP:EDGE_COLS],
                             dst[E - EDGE_COLS + DUP:E].rearrange("(p t) -> p t", p=1)).then_inc(const_loaded, 16)
                sp.dma_start(dst_next[P - 1:P, 0:EDGE_COLS - 1],
                             dst[E - EDGE_COLS + 1:E].rearrange("(p t) -> p t", p=1)).then_inc(const_loaded, 16)

            run_turns(sp, TURNS, turn)
            end = Turn(sp, TURNS // RING, 0)
            for n in range(RING - 1, 0, -1):
                store(end.back(n), R)
            store(end, R_LAST)
            sp.wait_ge(rest_ready, 1)
            sp.dma_start(out[P * NODE_ROWS:N, :], rest[0:REST, 5, :]).then_inc(rest_stored, 16)

        CONST_LOADED = 16 * (4 + 6 + 6)
        IDX_LOADED = 16 * 6

        @block.gpsimd
        def _(pool):
            nc.gpsimd.memset(idx[:, :, EDGE_COLS:], 0).then_inc(pads_set, 1)
            nc.gpsimd.memset(dst_once[:], int(BIG)).then_inc(pads_set, 1)
            nc.gpsimd.memset(dst_next[:], int(BIG)).then_inc(pads_set, 1)
            nc.gpsimd.memset(ident[:], 0.0).then_inc(const_made, 1)
            nc.gpsimd.memset(ones[:], 1.0).then_inc(const_made, 1)
            nc.gpsimd.memset(ln_eps[:], LN_EPS).then_inc(const_made, 1)
            nc.gpsimd.memset(goes_on[:, 0:1], 0.0).then_inc(const_made, 1)
            nc.gpsimd.memset(run[:, RING - 1, G - 1, :], 0.0).then_inc(const_made, 1)
            pool.wait_ge(const_made, 5)
            nc.gpsimd.affine_select(out=ident[:], in_=ident[:], compare_op=ALU.not_equal, fill=1.0, base=0,
                                    pattern=[[-1, P]], channel_multiplier=1).then_inc(const_made, 1)
            nc.gpsimd.affine_select(out=lower[:], in_=ones[:], compare_op=ALU.is_gt, fill=0.0, base=0,
                                    pattern=[[-1, P]], channel_multiplier=1).then_inc(const_made, 1)

            def gathers(t):
                wait_turn(pool, y_ready, t.back(RING))
                wait_turn(pool, idx_staged, t)
                pool.sem_inc(waited, 1)
                for tile in range(G):
                    for side in range(2):
                        pool.indirect_dma_start(
                            out=xin[:, t.j, R + 2 * tile + side, :], out_offset=None, in_=x,
                            in_offset=bass.IndirectOffsetOnAxis(ap=gather_idx[:, t.j, side, tile:tile + 1], axis=0),
                        ).then_inc(gathered[t.j], 16)

            run_turns(pool, TURNS, gathers)

            end = Turn(pool, TURNS // RING, 0)
            for n in range(RING):
                wait_slot(pool, y_stored, end.back(n), 1)
            pool.wait_ge(rest_stored, 16)

            last_row = pool.snap(pool.to_reg(N - 1))

            def add_rows(values, index):
                return pool.indirect_dma_start(
                    out=out, out_offset=bass.IndirectOffsetOnAxis(ap=index, axis=0), in_=values, in_offset=None,
                    bounds_check=last_row, oob_is_err=False, compute_op=ALU.add)

            def scatter(t):
                wait_turn(pool, sidx_staged, t)
                for tile in range(G):
                    if t.is_number(TURNS - 1) and tile == G - 1:
                        continue
                    wait_turn(pool, run_step, t, G, G - 1 - tile)
                    pool.sem_inc(waited, 1)
                    add_rows(run[:, t.j, tile, :], scatter_idx[:, t.j, tile:tile + 1]).then_inc(scattered[t.j], 16)

            run_turns(pool, TURNS, scatter)
            for n in range(1, RING):
                wait_slot(pool, scattered, end.back(n), G)
            pool.wait_ge(scattered[end.j], end.count(16 * G) - 16)

            with pool.If(pool.value_load(unsorted[0:1, 0:1], min_val=0, max_val=E)):
                with pool.Fori(0, EDGE_COLS - 1) as t:
                    pool.wait_ge(each["total"], pool.snap(t + 1))
                    pool.wait_ge(each["idx"], pool.snap(t + 1))
                    pool.sem_inc(waited, 1)
                    add_rows(total[:], once_idx[:]).then_inc(each["added"], 16)
                    pool.wait_ge(each["added"], pool.snap(16 * t + 16))
            pool.wait_ge(tail["total"], 1)
            pool.wait_ge(tail["idx"], 1)
            add_rows(total[:], once_idx[:]).then_inc(tail["added"], 16)
            pool.wait_ge(tail["added"], 16)

        CONST_MADE = 7
        @block.scalar
        def _(act):
            def stage_idx(t):
                nc.scalar.copy(gather_idx[:, t.j, :, :], idx[:, :, bass.ds(t.at(G), G)]).then_inc(idx_staged, 1)

            act.wait_ge(idx_loaded, IDX_LOADED)
            act.wait_ge(pads_set, 3)
            for j in range(RING):
                stage_idx(Turn(act, 0, j))
            act.wait_ge(w_turned, 1)
            nc.scalar.copy(wt_nodes[:], w_ps[:, 0:C]).then_inc(w_ready, 1)
            nc.scalar.copy(wt_edge[:], w_ps[0:D, C:2 * C]).then_inc(w_ready, 1)
            act.wait_ge(rest_var, 1)
            act.wait_ge(const_made, CONST_MADE)
            nc.scalar.activation(rest_c[0:REST, 3:4], rest_c[0:REST, 2:3], ACT.Sqrt, bias=ln_eps[0:REST, :],
                                 scale=1.0 / D).then_inc(rest_std, 1)

            def products(t):
                if not t.exists():
                    return
                b = t.j % 2
                wait_turn(act, rows_turned, t)
                wait_turn(act, multiplied, t.back(2))
                nc.scalar.copy(zt[:, b, :], zt_ps[b][:]).then_inc(zt_copied, 1)
                nc.scalar.copy(et[:, b, :], et_ps[b][0:D, :]).then_inc(et_copied, 1)

            def keep_pre(t):
                if not t.exists():
                    return
                wait_turn(act, multiplied, t)
                act.wait_ge(const_loaded, CONST_LOADED)
                nc.scalar.activation(pre[:, bass.ds(t.at(G * P), G * P)], pre_ps[t.j % 2][:], ACT.Identity,
                                     bias=bias[:], scale=1.0).then_inc(pre_copied, 1)

            def turn(t):
                b = t.j % 2
                wait_turn(act, var_ready, t.back(1))
                wait_turn(act, centred, t)
                nc.scalar.activation(sq[:], xc[:, b], ACT.Square).then_inc(squared, 1)
                if not t.is_number(TURNS - 1):
                    act.wait_ge(idx_loaded, IDX_LOADED)
                    stage_idx(t.back(-RING))
                products(t.back(1))
                wait_turn(act, var_ready, t)
                nc.scalar.activation(std[:, b, :], var[:, b, :], ACT.Sqrt, bias=ln_eps[:], scale=1.0 / D).then_inc(std_ready, 1)
                keep_pre(t.back(1))

            run_turns(act, TURNS, turn)
            end = Turn(act, TURNS // RING, 0)
            products(end)
            keep_pre(end)

            act.wait_ge(bn_var, 1)
            nc.scalar.activation(bn[:, 0:1], moments[:, 1:2], ACT.Sqrt, bias=ln_eps[:], scale=1.0).then_inc(bn_std, 1)

            def keep_runs(t):
                if not t.exists():
                    return
                wait_turn(act, run_step, t, G)
                act.wait_ge(bn_var, 1)
                nc.scalar.copy(pre[:, bass.ds(t.at(G * P), G * D)],
                               run[:, t.j, :, :].rearrange("p t d -> p (t d)")).then_inc(run_kept, 1)

            def exponentials(t):
                b = t.j % 2
                edges = zt_ps[b][:].rearrange("p (t c) -> p t c", t=G)
                wait_turn(act, act_turned, t)
                wait_turn(act, one_added, t.back(2))
                nc.scalar.activation(e_gate[:, b], edges[:, :, 0:D], ACT.Exp).then_inc(gate_exp, 1)
                nc.scalar.activation(c_abs[:, b], edges[:, :, D:C], ACT.Abs).then_inc(abs_done, 1)
                wait_turn(act, abs_done, t)
                nc.scalar.activation(e_core[:, b], c_abs[:, b], ACT.Exp, scale=-1.0).then_inc(core_exp, 1)
                wait_turn(act, core_exp, t)
                wait_turn(act, signal_ready, t.back(2))
                nc.scalar.activation(log1p[:, b], e_core[:, b], ACT.Ln, bias=ones[:, 0:1], scale=1.0).then_inc(log_done, 1)
                keep_runs(t.back(1))

            run_turns(act, TURNS, exponentials)
            keep_runs(end)

        @block.tensor
        def _(pe):
            def combine(s, n):
                pe.wait_ge(s["keys"], n)
                nc.tensor.transpose(k_ps[:, 0:P], keys[:], ident[:]).then_inc(s["turned"], 1)
                pe.wait_ge(s["equal"], n)
                pe.wait_ge(s["part"], n)
                nc.tensor.matmul(w_ps[:, 0:D], equal[:], part[:], start=True, stop=True).then_inc(s["summed"], 1)

            pe.wait_ge(const_made, CONST_MADE)
            pe.wait_ge(const_loaded, CONST_LOADED)
            nc.tensor.transpose(w_ps[:, 0:C], w_cat[:], ident[:])
            nc.tensor.transpose(w_ps[0:D, C:2 * C], w_edge[:], ident[:]).then_inc(w_turned, 1)
            pe.wait_ge(falls_ready, 1)
            nc.tensor.matmul(k_ps[:, 0:1], ones[:], nfalls[:], start=True, stop=True).then_inc(falls_summed, 1)
            pe.wait_ge(w_ready, 2)

            def turn(t):
                b = t.j % 2
                wait_turn(pe, zt_copied, t.back(2))
                wait_turn(pe, et_copied, t.back(2))
                wait_slot(pe, edges_loaded, t, 3)
                wait_turn(pe, h_ready, t)
                for tile in range(G):
                    nc.tensor.transpose(
                        zt_ps[b][:, tile * P:(tile + 1) * P],
                        h[:, b, R + 2 * tile:R + 2 * tile + 2, :].rearrange("p t d -> p (t d)"), ident[:])
                for tile in range(G):
                    last = nc.tensor.transpose(et_ps[b][0:D, tile * P:(tile + 1) * P], edge[:, t.j, tile, :],
                                               ident[:])
                last.then_inc(rows_turned, 1)
                wait_turn(pe, zt_copied, t)
                wait_turn(pe, pre_copied, t.back(2))
                wait_turn(pe, counted, t.back(2))
                nc.tensor.matmul(pre_ps[b][:], wt_nodes[:], zt[:, b, :], start=True, stop=False)
                wait_turn(pe, et_copied, t)
                pe.wait_ge(const_made, CONST_MADE)
                nc.tensor.matmul(pre_ps[b][:], wt_edge[:], et[:, b, :], start=False, stop=True).then_inc(
                    multiplied, 1)

            run_turns(pe, TURNS, turn)

            def turn_activations(t):
                b = t.j % 2
                wait_turn(pe, signal_ready, t.back(2))
                wait_turn(pe, affine_done, t)
                pe.wait_ge(const_made, CONST_MADE)
                for tile in range(G):
                    at = slice(tile * P, (tile + 1) * P)
                    last = nc.tensor.transpose(zt_ps[b][:, at], an[:, b, at], ident[:])
                last.then_inc(act_turned, 1)

            run_turns(pe, TURNS, turn_activations)

            pe.wait_ge(runs_ready, 1)
            with pe.If(pe.value_load(unsorted[0:1, 0:1], min_val=0, max_val=E)):
                with pe.Fori(0, EDGE_COLS - 1) as t:
                    combine(each, pe.snap(t + 1))
            combine(tail, 1)

        @block.vector
        def _(dve):
            links = [0]

            def linked(instruction):
                links[0] += 1
                instruction.then_inc(link, 1)
                dve.wait_ge(link, links[0])

            V = nc.vector

            def per_row(col):
                return col.unsqueeze(2).to_broadcast([P, ROWS, D])

            dve.wait_ge(const_loaded, CONST_LOADED)
            dve.wait_ge(idx_loaded, IDX_LOADED)
            dve.wait_ge(const_made, CONST_MADE)
            linked(V.tensor_tensor(falls[:], dst_next[:], idx[:, 0, 0:EDGE_COLS], ALU.is_lt))
            V.reduce_sum(nfalls[:], falls[:], axis=AX_X).then_inc(falls_ready, 1)
            linked(V.tensor_tensor(same[:], dst_next[:], dst_once[:], ALU.is_equal))
            linked(V.tensor_copy(dst_f[:], dst_once[:]))
            dve.wait_ge(falls_summed, 1)
            linked(V.tensor_scalar(is_sorted[:], k_ps[:, 0:1], 0.0, None, ALU.is_equal))
            linked(V.tensor_copy(unsorted[:], k_ps[:, 0:1]))
            linked(V.tensor_scalar(goes_on[:, 1:EDGE_COLS], same[:, 0:EDGE_COLS - 1], is_sorted[:], None, ALU.mult))
            linked(V.tensor_scalar(falls[:], same[:], -1.0, 1.0, ALU.mult, ALU.add))
            linked(V.tensor_scalar(same[:], falls[:], is_sorted[:], -BIG, ALU.mult, ALU.mult))
            V.scalar_tensor_tensor(run_idx[:], same[:], BIG, dst_f[:], ALU.add, ALU.add).then_inc(runs_ready, 1)

            r = slice(0, REST)
            dve.wait_ge(rest_loaded, 16)
            linked(V.reduce_sum(rest_c[r, 0:1], rest[r, 0, :], axis=AX_X))
            linked(V.tensor_scalar(rest_c[r, 1:2], rest_c[r, 0:1], 1.0 / D, None, ALU.mult))
            linked(V.tensor_scalar(rest[r, 1, :], rest[r, 0, :], rest_c[r, 1:2], None, ALU.subtract))
            linked(V.tensor_tensor(rest[r, 2, :], rest[r, 1, :], rest[r, 1, :], ALU.mult))
            V.reduce_sum(rest_c[r, 2:3], rest[r, 2, :], axis=AX_X).then_inc(rest_var, 1)
            dve.wait_ge(rest_std, 1)
            linked(V.reciprocal(rest_c[r, 4:5], rest_c[r, 3:4]))
            linked(V.tensor_scalar(rest[r, 3, :], rest[r, 1, :], 0.0, rest_c[r, 4:5], ALU.max, ALU.mult))
            V.tensor_tensor(rest[r, 5, :], rest[r, 3, :], rest[r, 0, :], ALU.add).then_inc(rest_ready, 1)

            def centre(t):
                b = t.j % 2
                wait_slot(dve, gathered, t, 2 * G)
                wait_slot(dve, nodes_loaded, t, 1)
                V.reduce_sum(xsum[:, b, :], xin[:, t.j], axis=AX_X).then_inc(summed, 1)
                wait_turn(dve, summed, t)
                V.scalar_tensor_tensor(xc[:, b], per_row(xsum[:, b, :]), -1.0 / D, xin[:, t.j], ALU.mult,
                                       ALU.add).then_inc(centred, 1)

            def variance(t):
                wait_turn(dve, squared, t)
                V.reduce_sum(var[:, t.j % 2, :], sq[:], axis=AX_X).then_inc(var_ready, 1)

            def normalise(t):
                if not t.exists():
                    return
                b = t.j % 2
                wait_turn(dve, std_ready, t)
                V.reciprocal(rstd[:, b, :], std[:, b, :]).then_inc(rstd_ready, 1)
                wait_turn(dve, rows_turned, t.back(2))
                wait_turn(dve, rstd_ready, t)
                V.scalar_tensor_tensor(h[:, b], xc[:, b], 0.0, per_row(rstd[:, b, :]), ALU.max,
                                       ALU.mult).then_inc(h_ready, 1)
                wait_slot(dve, y_stored, t.back(2), 1)
                wait_turn(dve, h_ready, t)
                V.tensor_tensor(y[:, b], h[:, b, 0:R, :], xin[:, t.j, 0:R, :], ALU.add).then_inc(y_ready, 1)

            def count_stats(t):
                if not t.exists():
                    return
                wait_turn(dve, pre_copied, t)
                dve.wait_ge(const_made, CONST_MADE)
                cols = pre[:, bass.ds(t.at(G * P), G * P)].rearrange("c (t p) -> c t p", t=G)
                V.bn_stats(stats[:, bass.ds(t.at(1), 1), :], cols[:, :, 0:P - 1]).then_inc(counted, 1)

            def turn(t):
                centre(t)
                normalise(t.back(1))
                variance(t)
                count_stats(t.back(2))

            run_turns(dve, TURNS, turn)
            end = Turn(dve, TURNS // RING, 0)
            normalise(end)
            count_stats(end.back(1))
            count_stats(end)
            last_cols = pre[:].rearrange("c (t p) -> c t p", p=P)[:, DUP:EDGE_COLS, P - 1]
            linked(V.bn_stats(stats[:, TURNS, :], last_cols))
            wait_turn(dve, counted, end)
            V.bn_aggr(moments[:], stats[:]).then_inc(bn_var, 1)
            dve.wait_ge(bn_std, 1)
            linked(V.reciprocal(bn[:, 1:2], bn[:, 0:1]))
            scale, shift = bn[:, 2:3], bn[:, 4:5]
            linked(V.tensor_tensor(scale, bn[:, 1:2], gamma[:], ALU.mult))
            linked(V.tensor_tensor(bn[:, 3:4], moments[:, 0:1], scale, ALU.mult))
            linked(V.tensor_tensor(shift, beta[:], bn[:, 3:4], ALU.subtract))
            linked(V.tensor_scalar(bn[0:D, 2:3], bn[0:D, 2:3], -1.0, None, ALU.mult))
            linked(V.tensor_scalar(bn[0:D, 4:5], bn[0:D, 4:5], -1.0, None, ALU.mult))

            def affine(t):
                wait_turn(dve, act_turned, t.back(2))
                dve.wait_ge(const_made, CONST_MADE)
                V.tensor_scalar(an[:, t.j % 2, :], pre[:, bass.ds(t.at(G * P), G * P)], scale, shift, ALU.mult,
                                ALU.add).then_inc(affine_done, 1)

            def messages(t):
                b = t.j % 2
                core = zt_ps[b][:].rearrange("p (t c) -> p t c", t=G)[:, :, D:C]
                wait_turn(dve, gate_exp, t)
                V.tensor_scalar(den[:], e_gate[:, b], 1.0, None, ALU.add).then_inc(one_added, 1)
                wait_turn(dve, one_added, t)
                V.reciprocal(gate[:], den[:]).then_inc(gate_ready, 1)
                wait_turn(dve, log_done, t)
                V.scalar_tensor_tensor(signal[:], core, 0.0, log1p[:, b], ALU.max, ALU.add).then_inc(signal_ready, 1)
                wait_slot(dve, scattered, t.back(RING), G)
                dve.wait_ge(const_made, CONST_MADE)
                V.tensor_copy(scatter_idx[:, t.j, :], run_idx[:, bass.ds(t.at(G), G)]).then_inc(sidx_staged, 1)
                V.tensor_copy(goes_now[:, t.j, :], goes_on[:, bass.ds(t.at(G), G)]).then_inc(goes_staged, 1)
                wait_turn(dve, gate_ready, t)
                wait_turn(dve, signal_ready, t)
                V.tensor_tensor(msg[:], signal[:], gate[:], ALU.mult).then_inc(msg_ready, 1)
                wait_turn(dve, run_kept, t.back(RING))
                wait_turn(dve, goes_staged, t)
                wait_turn(dve, msg_ready, t)
                for tile in range(G):
                    if tile:
                        before = run[:, t.j, tile - 1, :]
                        wait_turn(dve, run_step, t, G, G - tile)
                    else:
                        before = run[:, (t.j - 1) % RING, G - 1, :]
                        wait_turn(dve, run_step, t.back(1), G)
                    V.scalar_tensor_tensor(run[:, t.j, tile, :], before, goes_now[:, t.j, tile:tile + 1],
                                           msg[:, tile, :], ALU.mult, ALU.add).then_inc(run_step, 1)

            def turn2(t):
                if not t.is_number(TURNS - 1):
                    affine(t.back(-1))
                messages(t)

            affine(Turn(dve, 0, 0))
            run_turns(dve, TURNS, turn2)

            def combine(s, n, values, index):
                V.tensor_copy(key[:], index).then_inc(s["key"], 1)
                V.tensor_copy(part[:], values).then_inc(s["part"], 1)
                dve.wait_ge(s["key"], n)
                V.tensor_copy(keys[:], key[:].to_broadcast([P, P])).then_inc(s["keys"], 1)
                dve.wait_ge(s["turned"], n)
                V.tensor_scalar(equal[:], k_ps[:, 0:P], key[:], None, ALU.is_equal).then_inc(s["equal"], 1)
                dve.wait_ge(s["equal"], n)
                V.tensor_tensor(earlier[:], equal[:], lower[:], ALU.mult).then_inc(s["earlier"], 1)
                dve.wait_ge(s["earlier"], n)
                V.reduce_sum(repeats[:, 0:1], earlier[:], axis=AX_X).then_inc(s["counted"], 1)
                dve.wait_ge(s["counted"], n)
                V.tensor_scalar(repeats[:, 1:2], repeats[:, 0:1], 0.0, BIG, ALU.is_gt, ALU.mult).then_inc(
                    s["flagged"], 1)
                dve.wait_ge(s["flagged"], n)
                V.tensor_tensor(once_idx[:], repeats[:, 1:2], key[:], ALU.add).then_inc(s["idx"], 1)
                dve.wait_ge(s["summed"], n)
                V.tensor_copy(total[:], w_ps[:, 0:D]).then_inc(s["total"], 1)

            wait_turn(dve, run_kept, end)
            with dve.If(dve.value_load(unsorted[0:1, 0:1], min_val=0, max_val=E)):
                with dve.Fori(0, EDGE_COLS - 1) as t:
                    n = dve.snap(t + 1)
                    kept = (t // G) * (G * P) + (t % G) * D
                    combine(each, n, pre[:, bass.ds(kept, D)], dst_f[:, bass.ds(t, 1)])
                    dve.wait_ge(each["added"], dve.snap(16 * t + 16))
            combine(tail, 1, run[:, (TURNS - 1) % RING, G - 1, :], dst_f[:, EDGE_COLS - 1:EDGE_COLS])


_INS = ["x", "src", "dst", "edge_attr_64", "L0_gnn_W_filter", "L0_gnn_b_filter", "L0_gnn_gamma_filter",
        "L0_gnn_beta_filter", "L0_gnn_W_core", "L0_gnn_b_core", "L0_gnn_gamma_core", "L0_gnn_beta_core"]


def kernel(**inputs):
    import numpy as np
    import concourse.bacc as bacc
    from concourse.bass_utils import run_bass_kernel_spmd

    nc = bacc.Bacc("TRN2", target_bir_lowering=False, num_devices=1)
    arrays, args = {}, []
    for name in _INS:
        a = np.ascontiguousarray(inputs[name])
        arrays[f"in_{name}"] = a
        args.append(nc.dram_tensor(f"in_{name}", a.shape, mybir.dt.from_np(a.dtype), kind="ExternalInput").ap())
    out = nc.dram_tensor("out", arrays["in_x"].shape, F32, kind="ExternalOutput").ap()
    gnn_layer(nc, *args, out)
    r = run_bass_kernel_spmd(nc, [arrays], core_ids=[0])
    return r.results[0]["out"]
```

```python
from contextlib import ExitStack

import concourse.bass as bass
from concourse import mybir

F32 = mybir.dt.float32
I32 = mybir.dt.int32
ALU = mybir.AluOpType
ACT = mybir.ActivationFunctionType
AX_X = mybir.AxisListType.X
P = 128
RING = 4
BIG = float(1 << 20)
LN_EPS = 1e-5
BN_EPS = 1e-5


class Turn:

    def __init__(self, eng, i, j, shift=0, known=None):
        self.eng, self.i, self.j, self.shift, self.known = eng, i, j, shift, {} if known is None else known
        if isinstance(i, int):
            self.i, self.shift = i + shift, 0

    def back(self, n):
        at = self.j - n
        return Turn(self.eng, self.i, at % RING, self.shift + at // RING, self.known)

    def within(self, turns):
        return not isinstance(self.i, int) or 0 <= RING * self.i + self.j < turns

    def exists(self):
        return not isinstance(self.i, int) or self.i >= 0

    def is_number(self, k):
        return isinstance(self.i, int) and RING * self.i + self.j == k

    def linear(self, scale, add):
        if isinstance(self.i, int):
            return scale * self.i + add
        if (scale, add) not in self.known:
            self.known[scale, add] = self.eng.snap(self.i * scale + add)
        return self.known[scale, add]

    def count(self, unit):
        return self.linear(unit, unit * (self.shift + 1))

    def count_all(self, unit, short=0):
        return self.linear(unit * RING, unit * (RING * self.shift + self.j + 1) - short)

    def at(self, step):
        return self.linear(step * RING, step * (RING * self.shift + self.j))


def wait_turn(eng, semaphore, turn, unit=1, short=0):
    if turn.exists():
        eng.wait_ge(semaphore, turn.count_all(unit, short))


def wait_slot(eng, semaphores, turn, count):
    if turn.exists():
        eng.wait_ge(semaphores[turn.j], turn.count(16 * count))


def run_turns(eng, body, looped, turns):
    for j in range(RING):
        body(Turn(eng, 0, j))
    with eng.Fori(1, looped // RING) as i:
        known = {}
        for j in range(RING):
            body(Turn(eng, i, j, known=known))
    for k in range(looped // RING * RING, turns):
        body(Turn(eng, k // RING, k % RING))


def gnn_layer(nc, x, src, dst, edge_attr, w_filter, b_filter, g_filter, be_filter,
              w_core, b_core, g_core, be_core, out):
    N, D = x.shape
    E = edge_attr.shape[0]
    G = 4
    C = 2 * D
    EDGE_COLS = -(-E // P)
    TURNS = EDGE_COLS // G
    DUP = P * EDGE_COLS - E
    NODE_ROWS = N // P
    REST = N - P * NODE_ROWS
    R = -(-NODE_ROWS // (TURNS - 3))
    NODE_TURNS = -(-NODE_ROWS // R)
    R_LAST = NODE_ROWS - R * (NODE_TURNS - 1)
    assert D == 64 and C == P and EDGE_COLS % G == 0 and TURNS % RING == 1 and DUP < EDGE_COLS
    assert 0 < REST <= P
    PA = (P - 1) // 16 * 16
    CHUNKS = TURNS + 1

    x_rows = x[0:P * NODE_ROWS, :].rearrange("(p r) d -> p r d", p=P)
    out_rows = out[0:P * NODE_ROWS, :].rearrange("(p r) d -> p r d", p=P)
    edge_rows = edge_attr[0:(P - 1) * EDGE_COLS, :].rearrange("(p t) d -> p t d", p=P - 1)
    edge_last = edge_attr[E - EDGE_COLS:E, :].rearrange("(p t) d -> p t d", p=1)

    ctx = ExitStack()
    with ctx:
        def sb(name, shape, dt=F32):
            return ctx.enter_context(nc.sbuf_tensor(name, shape, dt))

        def sem(name):
            return ctx.enter_context(nc.semaphore(name))

        def sems(name):
            return [sem(f"{name}{j}") for j in range(RING)]

        ident = sb("ident", [P, P])
        lower = sb("lower", [P, P])
        ones = sb("ones", [P, P])
        w_cat = sb("w_cat", [P, 2 * D])
        w_edge = sb("w_edge", [P, D])
        wt_nodes = sb("wt_nodes", [P, C])
        wt_edge = sb("wt_edge", [D, C])
        bias = sb("bias", [P, 1])
        gamma = sb("gamma", [P, 1])
        beta = sb("beta", [P, 1])
        ln_eps = sb("ln_eps", [P, 1])
        idx = sb("idx", [P, 2, EDGE_COLS + RING * G], I32)
        gather_idx = sb("gather_idx", [P, RING, 2, G], I32)
        dst_once = sb("dst_once", [P, EDGE_COLS], I32)
        dst_next = sb("dst_next", [P, EDGE_COLS], I32)
        same = sb("same", [P, EDGE_COLS])
        falls = sb("falls", [P, EDGE_COLS])
        dst_f = sb("dst_f", [P, EDGE_COLS])
        goes_now = sb("goes_now", [P, RING, G])
        run_idx = sb("run_idx", [P, EDGE_COLS], I32)
        goes_on = sb("goes_on", [P, EDGE_COLS])
        nfalls = sb("nfalls", [P, 1])
        is_sorted = sb("is_sorted", [P, 1])
        unsorted = sb("unsorted", [P, 1], I32)
        pre = sb("pre", [P, TURNS * G * P])
        nodes = sb("nodes", [P, RING, R, D])
        node_y = sb("node_y", [P, RING, R, D])
        node_sq = sb("node_sq", [P, R, D])
        node_sum = sb("node_sum", [P, 2, R])
        node_var = sb("node_var", [P, 2, R])
        node_ln = sb("node_ln", [P, R])
        node_v = sb("node_v", [P, 2, R])
        node_root = sb("node_root", [P, 2, R])
        newton = sb("newton", [P, 2, R])
        node_rstd = sb("node_rstd", [P, R])
        ends = sb("ends", [P, RING, G, 2, D])
        edge = sb("edge", [P, RING, G, D])
        mean_of = sb("mean_of", [P, P])
        centre_of = sb("centre_of", [P, P])
        ends_t = sb("ends_t", [P, 2, G * P])
        edge_t = sb("edge_t", [D, RING, G * P])
        ends_sq = sb("ends_sq", [P, G * P])
        ends_ln = sb("ends_ln", [P, G * P])
        ends_rstd = sb("ends_rstd", [P, 2, G * P])
        ends_h = sb("ends_h", [P, 2, G * P])
        stats = sb("stats", [P, CHUNKS, 6])
        rest = sb("rest", [P, 6, D])
        rest_c = sb("rest_c", [P, 8])
        moments = sb("moments", [P, 2])
        bn = sb("bn", [P, 8])
        neg_beta = sb("neg_beta", [P, 1])
        an = ends_t
        logs = ends_rstd[:].rearrange("p b (t c) -> p b t c", t=G)
        exps = ends_sq[:].rearrange("p (t c) -> p t c", t=G)
        spare = ends_h[:].rearrange("p b (t n d) -> p n b t d", t=G, n=2)
        gate = spare[:, 0]
        c_abs = spare[:, 1, 0]
        signal = sb("signal", [P, G, D])
        msg = sb("msg", [P, G, D])
        run = sb("run", [P, RING, G, D])
        scatter_idx = sb("scatter_idx", [P, RING, G], I32)
        key = sb("key", [P, 1])
        keys = sb("keys", [P, P])
        equal = sb("equal", [P, P])
        earlier = sb("earlier", [P, P])
        repeats = sb("repeats", [P, 2])
        once_idx = sb("once_idx", [P, 1], I32)
        part = sb("part", [P, D])
        total = sb("total", [P, D])

        def banks(name, shape):
            return [ctx.enter_context(nc.psum_tensor(f"{name}{b}", shape, F32)) for b in range(2)]

        turned_ps = banks("turned_ps", [P, G * P])
        centred_ps = banks("centred_ps", [P, G * P])
        pre_ps = banks("pre_ps", [P, G * P])
        edge_ps = ctx.enter_context(nc.psum_tensor("edge_ps", [P, G * P], F32))
        var_ps = ctx.enter_context(nc.psum_tensor("var_ps", [P, G * P], F32))
        w_ps, k_ps = centred_ps

        idx_loaded = sem("idx_loaded")
        const_loaded = sem("const_loaded")
        const_made = sem("const_made")
        waited = sem("waited")
        mean_cleared = sem("mean_cleared")
        pads_set = sem("pads_set")
        w_turned = sem("w_turned")
        w_ready = sem("w_ready")
        rest_loaded = sem("rest_loaded")
        rest_stored = sem("rest_stored")
        rest_var = sem("rest_var")
        rest_ready = sem("rest_ready")
        rest_ln = sem("rest_ln")
        rest_rstd = sem("rest_rstd")
        link = sem("link")
        bn_ready = sem("bn_ready")
        falls_ready = sem("falls_ready")
        falls_summed = sem("falls_summed")
        runs_ready = sem("runs_ready")
        idx_staged = sem("idx_staged")
        gathered = sems("gathered")
        nodes_loaded = sems("nodes_loaded")
        edges_loaded = sems("edges_loaded")
        node_summed = sem("node_summed")
        node_centred = sem("node_centred")
        node_squared = sem("node_squared")
        node_var_ready = sem("node_var_ready")
        node_ln_ready = sem("node_ln_ready")
        node_root_ready = sem("node_root_ready")
        newton_1 = sem("newton_1")
        newton_2 = sem("newton_2")
        node_rstd_ready = sem("node_rstd_ready")
        node_h_ready = sem("node_h_ready")
        y_ready = sem("y_ready")
        y_stored = sems("y_stored")
        centre_ready = sem("centre_ready")
        turned = sem("turned")
        ends_copied = sem("ends_copied")
        edge_copied = sem("edge_copied")
        centred = sem("centred")
        squared = sem("squared")
        var_done = sem("var_done")
        ln_ready = sem("ln_ready")
        rstd_ready = sem("rstd_ready")
        h_ready = sem("h_ready")
        multiplied = sem("multiplied")
        pre_copied = sem("pre_copied")
        counted = sem("counted")
        bn_var = sem("bn_var")
        bn_ln = sem("bn_ln")
        bn_rstd = sem("bn_rstd")
        affine_done = sem("affine_done")
        act_turned = sem("act_turned")
        gate_exp = sem("gate_exp")
        abs_done = sem("abs_done")
        core_exp = sem("core_exp")
        log_done = sem("log_done")
        gate_ready = sem("gate_ready")
        signal_ready = sem("signal_ready")
        msg_ready = sem("msg_ready")
        run_step = sem("run_step")
        sidx_staged = sem("sidx_staged")
        goes_staged = sem("goes_staged")
        scattered = sems("scattered")
        run_kept = sem("run_kept")
        def combine_sems(name):
            return {s: sem(f"{name}_{s}") for s in
                    ("key", "keys", "turned", "equal", "earlier", "counted", "flagged", "idx", "part", "summed",
                     "total", "added")}
        tail = combine_sems("tail")
        each = combine_sems("each")

        block = ctx.enter_context(nc.Block())
        LOOPED = NODE_TURNS - 1
        CONST_LOADED = 16 * (4 + 6 + 6)
        IDX_LOADED = 16 * 6
        CONST_MADE = 9

        @block.sync
        def _(sp):
            sp.wait_ge(pads_set, 3)
            for k, table in enumerate((dst, src)):
                rows = table[0:(P - 1) * EDGE_COLS].rearrange("(p t) -> p t", p=P - 1)
                sp.dma_start(idx[0:PA, k, 0:EDGE_COLS], rows[0:PA, :]).then_inc(idx_loaded, 16)
                sp.dma_start(idx[PA:P - 1, k, 0:EDGE_COLS], rows[PA:P - 1, :]).then_inc(idx_loaded, 16)
                sp.dma_start(idx[P - 1:P, k, 0:EDGE_COLS],
                             table[E - EDGE_COLS:E].rearrange("(p t) -> p t", p=1)).then_inc(idx_loaded, 16)

            def loads(t):
                if t.within(NODE_TURNS):
                    rows = R_LAST if t.is_number(NODE_TURNS - 1) else R
                    wait_turn(sp, y_ready, t.back(RING))
                    sp.dma_start(nodes[:, t.j, 0:rows, :], x_rows[:, bass.ds(t.at(R), rows), :]).then_inc(
                        nodes_loaded[t.j], 16)
                if t.within(TURNS):
                    wait_turn(sp, turned, t.back(RING))
                    for d, s in ((edge[0:PA], edge_rows[0:PA]), (edge[PA:P - 1], edge_rows[PA:P - 1]),
                                 (edge[P - 1:P], edge_last)):
                        sp.dma_start(d[:, t.j, :, :], s[:, bass.ds(t.at(G), G), :]).then_inc(edges_loaded[t.j], 16)

            def store(t):
                if not t.within(NODE_TURNS):
                    return
                rows = R_LAST if t.is_number(NODE_TURNS - 1) else R
                wait_turn(sp, y_ready, t)
                sp.dma_start(out_rows[:, bass.ds(t.at(R), rows), :], node_y[:, t.j, 0:rows, :]).then_inc(
                    y_stored[t.j], 16)

            def turn(t):
                store(t.back(RING))
                loads(t)
                if t.is_number(1):
                    small_loads()

            def small_loads():
                sp.dma_start(rest[0:REST, 0, :], x[P * NODE_ROWS:N, :]).then_inc(rest_loaded, 16)
                for w, at in ((w_filter, 0), (w_core, D)):
                    sp.dma_start(w_cat[at:at + D, :], w[:, 0:2 * D]).then_inc(const_loaded, 16)
                    sp.dma_start(w_edge[at:at + D, :], w[:, 2 * D:3 * D]).then_inc(const_loaded, 16)
                for col, filt, core in ((bias, b_filter, b_core), (gamma, g_filter, g_core),
                                        (beta, be_filter, be_core)):
                    for v, at in ((filt, 0), (core, D)):
                        sp.dma_start(col[at:at + D, :], v.rearrange("(d o) -> d o", o=1)).then_inc(const_loaded, 16)
                rows = dst[0:(P - 1) * EDGE_COLS].rearrange("(p t) -> p t", p=P - 1)
                after = dst[1:(P - 1) * EDGE_COLS + 1].rearrange("(p t) -> p t", p=P - 1)
                for d, s in ((dst_once, rows), (dst_next, after)):
                    sp.dma_start(d[0:PA, :], s[0:PA, :]).then_inc(const_loaded, 16)
                    sp.dma_start(d[PA:P - 1, :], s[PA:P - 1, :]).then_inc(const_loaded, 16)
                sp.dma_start(dst_once[P - 1:P, DUP:EDGE_COLS],
                             dst[E - EDGE_COLS + DUP:E].rearrange("(p t) -> p t", p=1)).then_inc(const_loaded, 16)
                sp.dma_start(dst_next[P - 1:P, 0:EDGE_COLS - 1],
                             dst[E - EDGE_COLS + 1:E].rearrange("(p t) -> p t", p=1)).then_inc(const_loaded, 16)

            run_turns(sp, turn, LOOPED, TURNS + RING)
            sp.wait_ge(rest_ready, 1)
            sp.dma_start(out[P * NODE_ROWS:N, :], rest[0:REST, 5, :]).then_inc(rest_stored, 16)


        @block.gpsimd
        def _(pool):
            nc.gpsimd.memset(idx[:, :, EDGE_COLS:], 0).then_inc(pads_set, 1)
            nc.gpsimd.memset(dst_once[:], int(BIG)).then_inc(pads_set, 1)
            nc.gpsimd.memset(dst_next[:], int(BIG)).then_inc(pads_set, 1)
            nc.gpsimd.memset(ident[:], 0.0).then_inc(const_made, 1)
            nc.gpsimd.memset(ones[:], 1.0).then_inc(const_made, 1)
            nc.gpsimd.memset(ln_eps[:], LN_EPS).then_inc(const_made, 1)
            nc.gpsimd.memset(goes_on[:, 0:1], 0.0).then_inc(const_made, 1)
            nc.gpsimd.memset(run[:, RING - 1, G - 1, :], 0.0).then_inc(const_made, 1)
            nc.gpsimd.memset(mean_of[:], 0.0).then_inc(mean_cleared, 1)
            pool.wait_ge(mean_cleared, 1)
            for half in range(2):
                part_of = slice(half * D, (half + 1) * D)
                nc.gpsimd.memset(mean_of[part_of, part_of], 1.0 / D).then_inc(const_made, 1)
            pool.wait_ge(const_made, 7)
            nc.gpsimd.affine_select(out=ident[:], in_=ident[:], compare_op=ALU.not_equal, fill=1.0, base=0,
                                    pattern=[[-1, P]], channel_multiplier=1).then_inc(const_made, 1)
            nc.gpsimd.affine_select(out=lower[:], in_=ones[:], compare_op=ALU.is_gt, fill=0.0, base=0,
                                    pattern=[[-1, P]], channel_multiplier=1).then_inc(const_made, 1)

            def gathers(t):
                wait_turn(pool, turned, t.back(RING))
                wait_turn(pool, idx_staged, t)
                pool.sem_inc(waited, 1)
                for tile in range(G):
                    for side in range(2):
                        pool.indirect_dma_start(
                            out=ends[:, t.j, tile, side, :], out_offset=None, in_=x,
                            in_offset=bass.IndirectOffsetOnAxis(ap=gather_idx[:, t.j, side, tile:tile + 1], axis=0),
                        ).then_inc(gathered[t.j], 16)

            run_turns(pool, gathers, TURNS, TURNS)

            end = Turn(pool, TURNS // RING, 0)
            for n in range(RING):
                wait_slot(pool, y_stored, Turn(pool, 0, NODE_TURNS - 1).back(n), 1)
            pool.wait_ge(rest_stored, 16)

            last_row = pool.snap(pool.to_reg(N - 1))

            def add_rows(values, index):
                return pool.indirect_dma_start(
                    out=out, out_offset=bass.IndirectOffsetOnAxis(ap=index, axis=0), in_=values, in_offset=None,
                    bounds_check=last_row, oob_is_err=False, compute_op=ALU.add)

            def scatter(t):
                wait_turn(pool, sidx_staged, t)
                for tile in range(G):
                    if t.is_number(TURNS - 1) and tile == G - 1:
                        continue
                    wait_turn(pool, run_step, t, G, G - 1 - tile)
                    pool.sem_inc(waited, 1)
                    add_rows(run[:, t.j, tile, :], scatter_idx[:, t.j, tile:tile + 1]).then_inc(scattered[t.j], 16)

            run_turns(pool, scatter, TURNS, TURNS)
            for n in range(1, RING):
                wait_slot(pool, scattered, end.back(n), G)
            pool.wait_ge(scattered[end.j], end.count(16 * G) - 16)

            with pool.If(pool.value_load(unsorted[0:1, 0:1], min_val=0, max_val=E)):
                with pool.Fori(0, EDGE_COLS - 1) as t:
                    pool.wait_ge(each["total"], pool.snap(t + 1))
                    pool.wait_ge(each["idx"], pool.snap(t + 1))
                    pool.sem_inc(waited, 1)
                    add_rows(total[:], once_idx[:]).then_inc(each["added"], 16)
                    pool.wait_ge(each["added"], pool.snap(16 * t + 16))
            pool.wait_ge(tail["total"], 1)
            pool.wait_ge(tail["idx"], 1)
            add_rows(total[:], once_idx[:]).then_inc(tail["added"], 16)
            pool.wait_ge(tail["added"], 16)

        @block.scalar
        def _(act):
            def stage_idx(t):
                nc.scalar.copy(gather_idx[:, t.j, :, :], idx[:, :, bass.ds(t.at(G), G)]).then_inc(idx_staged, 1)

            nc.scalar.preload_act_table_set("natural_log_exp_and_others")
            act.wait_ge(idx_loaded, IDX_LOADED)
            act.wait_ge(pads_set, 3)
            for j in range(RING):
                stage_idx(Turn(act, 0, j))
            act.wait_ge(w_turned, 1)
            nc.scalar.copy(wt_nodes[:], w_ps[:, 0:C]).then_inc(w_ready, 1)
            nc.scalar.copy(wt_edge[:], w_ps[0:D, C:2 * C]).then_inc(w_ready, 1)

            act.wait_ge(rest_var, 1)
            act.wait_ge(const_made, CONST_MADE)
            nc.scalar.activation(rest_c[0:REST, 3:4], rest_c[0:REST, 2:3], ACT.Ln, bias=ln_eps[0:REST, :],
                                 scale=1.0 / D).then_inc(rest_ln, 1)
            act.wait_ge(rest_ln, 1)
            nc.scalar.activation(rest_c[0:REST, 4:5], rest_c[0:REST, 3:4], ACT.Exp, scale=-0.5).then_inc(rest_rstd, 1)

            def copy_turned(t):
                if not t.within(TURNS):
                    return
                wait_turn(act, centred, t.back(2))
                wait_turn(act, multiplied, t.back(RING))
                wait_turn(act, turned, t)
                nc.scalar.copy(ends_t[:, t.j % 2, :], turned_ps[t.j % 2][:]).then_inc(ends_copied, 1)
                nc.scalar.copy(edge_t[:, t.j, :], edge_ps[0:D, :]).then_inc(edge_copied, 1)
                if not t.is_number(TURNS - 1):
                    stage_idx(t.back(-RING))

            def root_ends(t):
                if not t.within(TURNS):
                    return
                wait_turn(act, h_ready, t.back(2))
                wait_turn(act, var_done, t)
                nc.scalar.activation(ends_ln[:], var_ps[:], ACT.Ln, bias=ln_eps[:], scale=1.0).then_inc(ln_ready, 1)
                wait_turn(act, ln_ready, t)
                nc.scalar.activation(ends_rstd[:, t.j % 2, :], ends_ln[:], ACT.Exp, scale=-0.5).then_inc(
                    rstd_ready, 1)

            def keep_pre(t):
                if not t.within(TURNS):
                    return
                wait_turn(act, multiplied, t)
                act.wait_ge(const_loaded, CONST_LOADED)
                nc.scalar.activation(pre[:, bass.ds(t.at(G * P), G * P)], pre_ps[t.j % 2][:], ACT.Identity,
                                     bias=bias[:], scale=1.0).then_inc(pre_copied, 1)

            def square_nodes(t):
                if not t.within(NODE_TURNS):
                    return
                wait_turn(act, node_var_ready, t.back(1))
                wait_turn(act, node_centred, t)
                nc.scalar.activation(node_sq[:], node_y[:, t.j], ACT.Square).then_inc(node_squared, 1)

            def square_ends(t):
                if not t.within(TURNS):
                    return
                wait_turn(act, var_done, t.back(1))
                wait_turn(act, centred, t)
                nc.scalar.activation(ends_sq[:], centred_ps[t.j % 2][:], ACT.Square).then_inc(squared, 1)

            def root_nodes(t):
                if not t.within(NODE_TURNS):
                    return
                b = t.j % 2
                wait_turn(act, node_h_ready, t.back(2))
                wait_turn(act, node_var_ready, t)
                nc.scalar.activation(node_ln[:], node_var[:, b, :], ACT.Ln, bias=ln_eps[:], scale=1.0 / D).then_inc(
                    node_ln_ready, 1)
                nc.scalar.activation(node_v[:, b, :], node_var[:, b, :], ACT.Identity, bias=ln_eps[:], scale=1.0 / D)
                wait_turn(act, node_ln_ready, t)
                nc.scalar.activation(node_root[:, b, :], node_ln[:], ACT.Exp, scale=-0.5).then_inc(
                    node_root_ready, 1)

            def turn(t):
                copy_turned(t)
                root_ends(t.back(1))
                keep_pre(t.back(2))
                square_nodes(t)
                square_ends(t)
                root_nodes(t)

            run_turns(act, turn, LOOPED, TURNS + 2)
            end = Turn(act, TURNS // RING, 0)

            act.wait_ge(bn_var, 1)
            nc.scalar.activation(bn[:, 0:1], moments[:, 1:2], ACT.Ln, bias=ln_eps[:], scale=1.0).then_inc(bn_ln, 1)
            act.wait_ge(bn_ln, 1)
            nc.scalar.activation(bn[:, 1:2], bn[:, 0:1], ACT.Exp, scale=-0.5).then_inc(bn_rstd, 1)

            def keep_runs(t):
                if not t.exists():
                    return
                wait_turn(act, run_step, t, G)
                act.wait_ge(bn_var, 1)
                nc.scalar.copy(pre[:, bass.ds(t.at(G * P), G * D)],
                               run[:, t.j, :, :].rearrange("p t d -> p (t d)")).then_inc(run_kept, 1)

            def exponentials(t):
                b = t.j % 2
                edges = turned_ps[b][:].rearrange("p (t c) -> p t c", t=G)
                wait_turn(act, act_turned, t)
                nc.scalar.activation(c_abs, edges[:, :, D:C], ACT.Abs).then_inc(abs_done, 1)
                wait_turn(act, log_done, t.back(1))
                nc.scalar.activation(exps[:, :, 0:D], edges[:, :, 0:D], ACT.Exp).then_inc(gate_exp, 1)
                wait_turn(act, abs_done, t)
                nc.scalar.activation(exps[:, :, D:C], c_abs, ACT.Exp, scale=-1.0).then_inc(core_exp, 1)
                wait_turn(act, gate_exp, t)
                wait_turn(act, core_exp, t)
                wait_turn(act, signal_ready, t.back(2))
                nc.scalar.activation(logs[:, b], exps[:], ACT.Ln, bias=ones[:, 0:1], scale=1.0).then_inc(log_done, 1)
                wait_turn(act, log_done, t)
                wait_turn(act, msg_ready, t.back(2))
                nc.scalar.activation(gate[:, b], logs[:, b, :, 0:D], ACT.Exp, scale=-1.0).then_inc(gate_ready, 1)
                keep_runs(t.back(1))

            run_turns(act, exponentials, TURNS, TURNS)
            keep_runs(end)

        @block.tensor
        def _(pe):
            def combine(s, n):
                pe.wait_ge(s["keys"], n)
                nc.tensor.transpose(k_ps[:, 0:P], keys[:], ident[:]).then_inc(s["turned"], 1)
                pe.wait_ge(s["equal"], n)
                pe.wait_ge(s["part"], n)
                nc.tensor.matmul(w_ps[:, 0:D], equal[:], part[:], start=True, stop=True).then_inc(s["summed"], 1)

            pe.wait_ge(const_made, CONST_MADE)
            pe.wait_ge(const_loaded, CONST_LOADED)
            nc.tensor.transpose(w_ps[:, 0:C], w_cat[:], ident[:])
            nc.tensor.transpose(w_ps[0:D, C:2 * C], w_edge[:], ident[:]).then_inc(w_turned, 1)
            pe.wait_ge(falls_ready, 1)
            nc.tensor.matmul(k_ps[:, 0:1], ones[:], nfalls[:], start=True, stop=True).then_inc(falls_summed, 1)
            pe.wait_ge(w_ready, 2)

            pe.wait_ge(centre_ready, 1)

            def turn_rows(t):
                if not t.within(TURNS):
                    return
                b = t.j % 2
                wait_turn(pe, ends_copied, t.back(2))
                wait_turn(pe, edge_copied, t.back(1))
                wait_slot(pe, edges_loaded, t, 3)
                wait_slot(pe, gathered, t, 2 * G)
                for tile in range(G):
                    nc.tensor.transpose(turned_ps[b][:, tile * P:(tile + 1) * P],
                                        ends[:, t.j, tile].rearrange("p s d -> p (s d)"), ident[:])
                for tile in range(G):
                    last = nc.tensor.transpose(edge_ps[0:D, tile * P:(tile + 1) * P], edge[:, t.j, tile, :],
                                               ident[:])
                last.then_inc(turned, 1)

            def centre(t):
                if not t.within(TURNS):
                    return
                wait_turn(pe, h_ready, t.back(2))
                wait_turn(pe, ends_copied, t)
                nc.tensor.matmul(centred_ps[t.j % 2][:], centre_of[:], ends_t[:, t.j % 2, :], start=True,
                                 stop=True).then_inc(centred, 1)

            def variance(t):
                if not t.within(TURNS):
                    return
                wait_turn(pe, ln_ready, t.back(1))
                wait_turn(pe, squared, t)
                nc.tensor.matmul(var_ps[:], mean_of[:], ends_sq[:], start=True, stop=True).then_inc(var_done, 1)

            def product(t):
                if not t.within(TURNS):
                    return
                b = t.j % 2
                wait_turn(pe, pre_copied, t.back(2))
                wait_turn(pe, edge_copied, t)
                wait_turn(pe, h_ready, t)
                nc.tensor.matmul(pre_ps[b][:], wt_nodes[:], ends_h[:, b, :], start=True, stop=False)
                nc.tensor.matmul(pre_ps[b][:], wt_edge[:], edge_t[:, t.j, :], start=False, stop=True).then_inc(
                    multiplied, 1)

            def turn(t):
                turn_rows(t)
                variance(t.back(1))
                product(t.back(2))
                centre(t)

            run_turns(pe, turn, LOOPED, TURNS + 2)

            def turn_activations(t):
                b = t.j % 2
                wait_turn(pe, signal_ready, t.back(2))
                wait_turn(pe, affine_done, t)
                pe.wait_ge(const_made, CONST_MADE)
                for tile in range(G):
                    at = slice(tile * P, (tile + 1) * P)
                    last = nc.tensor.transpose(turned_ps[b][:, at], an[:, b, at], ident[:])
                last.then_inc(act_turned, 1)

            run_turns(pe, turn_activations, TURNS, TURNS)

            pe.wait_ge(runs_ready, 1)
            with pe.If(pe.value_load(unsorted[0:1, 0:1], min_val=0, max_val=E)):
                with pe.Fori(0, EDGE_COLS - 1) as t:
                    combine(each, pe.snap(t + 1))
            combine(tail, 1)

        @block.vector
        def _(dve):
            links = [0]

            def linked(instruction):
                links[0] += 1
                instruction.then_inc(link, 1)
                dve.wait_ge(link, links[0])

            V = nc.vector

            def per_row(col):
                return col.unsqueeze(2).to_broadcast([P, R, D])

            dve.wait_ge(const_loaded, CONST_LOADED)
            dve.wait_ge(idx_loaded, IDX_LOADED)
            dve.wait_ge(const_made, CONST_MADE)
            V.tensor_tensor(centre_of[:], ident[:], mean_of[:], ALU.subtract).then_inc(centre_ready, 1)
            linked(V.tensor_tensor(falls[:], dst_next[:], idx[:, 0, 0:EDGE_COLS], ALU.is_lt))
            V.reduce_sum(nfalls[:], falls[:], axis=AX_X).then_inc(falls_ready, 1)
            linked(V.tensor_tensor(same[:], dst_next[:], dst_once[:], ALU.is_equal))
            linked(V.tensor_copy(dst_f[:], dst_once[:]))
            dve.wait_ge(falls_summed, 1)
            linked(V.tensor_scalar(is_sorted[:], k_ps[:, 0:1], 0.0, None, ALU.is_equal))
            linked(V.tensor_copy(unsorted[:], k_ps[:, 0:1]))
            linked(V.tensor_scalar(goes_on[:, 1:EDGE_COLS], same[:, 0:EDGE_COLS - 1], is_sorted[:], None, ALU.mult))
            linked(V.tensor_scalar(falls[:], same[:], -1.0, 1.0, ALU.mult, ALU.add))
            linked(V.tensor_scalar(same[:], falls[:], is_sorted[:], -BIG, ALU.mult, ALU.mult))
            V.scalar_tensor_tensor(run_idx[:], same[:], BIG, dst_f[:], ALU.add, ALU.add).then_inc(runs_ready, 1)

            r = slice(0, REST)
            dve.wait_ge(rest_loaded, 16)
            linked(V.reduce_sum(rest_c[r, 0:1], rest[r, 0, :], axis=AX_X))
            linked(V.tensor_scalar(rest_c[r, 1:2], rest_c[r, 0:1], 1.0 / D, None, ALU.mult))
            linked(V.tensor_scalar(rest[r, 1, :], rest[r, 0, :], rest_c[r, 1:2], None, ALU.subtract))
            linked(V.tensor_tensor(rest[r, 2, :], rest[r, 1, :], rest[r, 1, :], ALU.mult))
            V.reduce_sum(rest_c[r, 2:3], rest[r, 2, :], axis=AX_X).then_inc(rest_var, 1)
            dve.wait_ge(rest_rstd, 1)
            v, root = rest_c[r, 5:6], rest_c[r, 4:5]
            linked(V.tensor_scalar(v, rest_c[r, 2:3], 1.0 / D, LN_EPS, ALU.mult, ALU.add))
            linked(V.tensor_scalar(rest_c[r, 6:7], v, root, root, ALU.mult, ALU.mult))
            linked(V.tensor_scalar(rest_c[r, 6:7], rest_c[r, 6:7], -0.5, 1.5, ALU.mult, ALU.add))
            linked(V.tensor_scalar(rest_c[r, 7:8], rest_c[r, 6:7], root, None, ALU.mult))
            linked(V.tensor_scalar(rest[r, 3, :], rest[r, 1, :], 0.0, rest_c[r, 7:8], ALU.max, ALU.mult))
            V.tensor_tensor(rest[r, 5, :], rest[r, 3, :], rest[r, 0, :], ALU.add).then_inc(rest_ready, 1)

            linked(V.tensor_scalar(gamma[0:D, :], gamma[0:D, :], -1.0, None, ALU.mult))
            linked(V.tensor_scalar(neg_beta[:], beta[:], -1.0, None, ALU.mult))
            linked(V.tensor_scalar(neg_beta[0:D, :], beta[0:D, :], 1.0, None, ALU.mult))

            def centre_nodes(t):
                if not t.within(NODE_TURNS):
                    return
                b = t.j % 2
                wait_slot(dve, nodes_loaded, t, 1)
                V.reduce_sum(node_sum[:, b, :], nodes[:, t.j], axis=AX_X).then_inc(node_summed, 1)
                wait_slot(dve, y_stored, t.back(RING), 1)
                wait_turn(dve, node_summed, t)
                V.scalar_tensor_tensor(node_y[:, t.j], per_row(node_sum[:, b, :]), -1.0 / D, nodes[:, t.j], ALU.mult,
                                       ALU.add).then_inc(node_centred, 1)

            def variance_nodes(t):
                if not t.within(NODE_TURNS):
                    return
                wait_turn(dve, node_squared, t)
                V.reduce_sum(node_var[:, t.j % 2, :], node_sq[:], axis=AX_X).then_inc(node_var_ready, 1)

            def normalise_nodes(t):
                if not t.within(NODE_TURNS):
                    return
                root, v = node_root[:, t.j % 2, :], node_v[:, t.j % 2, :]
                wait_turn(dve, node_root_ready, t)
                V.tensor_tensor(newton[:, 0, :], v, root, ALU.mult).then_inc(newton_1, 1)
                wait_turn(dve, newton_1, t)
                V.scalar_tensor_tensor(newton[:, 1, :], newton[:, 0, :], -0.5, root, ALU.mult, ALU.mult).then_inc(
                    newton_2, 1)
                wait_turn(dve, newton_2, t)
                V.scalar_tensor_tensor(node_rstd[:], newton[:, 1, :], 1.5, root, ALU.add, ALU.mult).then_inc(
                    node_rstd_ready, 1)
                wait_turn(dve, node_rstd_ready, t)
                V.scalar_tensor_tensor(node_y[:, t.j], node_y[:, t.j], 0.0, per_row(node_rstd[:]), ALU.max,
                                       ALU.mult).then_inc(node_h_ready, 1)
                wait_turn(dve, node_h_ready, t)
                V.tensor_tensor(node_y[:, t.j], node_y[:, t.j], nodes[:, t.j], ALU.add).then_inc(y_ready, 1)

            def normalise_ends(t):
                if not t.within(TURNS):
                    return
                b = t.j % 2
                wait_turn(dve, multiplied, t.back(2))
                wait_turn(dve, rstd_ready, t)
                V.scalar_tensor_tensor(ends_h[:, b, :], centred_ps[b][:], 0.0, ends_rstd[:, b, :], ALU.max,
                                       ALU.mult).then_inc(h_ready, 1)

            def count_stats(t):
                if not t.within(TURNS):
                    return
                wait_turn(dve, pre_copied, t)
                dve.wait_ge(const_made, CONST_MADE)
                cols = pre[:, bass.ds(t.at(G * P), G * P)].rearrange("c (t p) -> c t p", t=G)
                V.bn_stats(stats[:, bass.ds(t.at(1), 1), :], cols[:, :, 0:P - 1]).then_inc(counted, 1)

            def turn(t):
                centre_nodes(t)
                normalise_ends(t.back(1))
                normalise_nodes(t.back(1))
                variance_nodes(t)
                count_stats(t.back(3))

            run_turns(dve, turn, LOOPED, TURNS + 3)
            end = Turn(dve, TURNS // RING, 0)
            last_cols = pre[:].rearrange("c (t p) -> c t p", p=P)[:, DUP:EDGE_COLS, P - 1]
            linked(V.bn_stats(stats[:, TURNS, :], last_cols))
            wait_turn(dve, counted, end)
            V.bn_aggr(moments[:], stats[:]).then_inc(bn_var, 1)
            dve.wait_ge(bn_rstd, 1)
            root, v, scale, shift = bn[:, 1:2], bn[:, 2:3], bn[:, 5:6], bn[:, 6:7]
            linked(V.tensor_scalar(v, moments[:, 1:2], BN_EPS, root, ALU.add, ALU.mult))
            linked(V.tensor_scalar(bn[:, 3:4], v, root, -0.5, ALU.mult, ALU.mult))
            linked(V.tensor_scalar(bn[:, 4:5], bn[:, 3:4], 1.5, root, ALU.add, ALU.mult))
            linked(V.tensor_tensor(scale, bn[:, 4:5], gamma[:], ALU.mult))
            linked(V.scalar_tensor_tensor(shift, moments[:, 0:1], scale, neg_beta[:], ALU.mult, ALU.add))
            linked(V.tensor_scalar(shift, shift, -1.0, None, ALU.mult))

            def affine(t):
                wait_turn(dve, act_turned, t.back(2))
                dve.wait_ge(const_made, CONST_MADE)
                V.tensor_scalar(an[:, t.j % 2, :], pre[:, bass.ds(t.at(G * P), G * P)], scale, shift, ALU.mult,
                                ALU.add).then_inc(affine_done, 1)

            def messages(t):
                b = t.j % 2
                core = turned_ps[b][:].rearrange("p (t c) -> p t c", t=G)[:, :, D:C]
                wait_turn(dve, log_done, t)
                V.scalar_tensor_tensor(signal[:], core, 0.0, logs[:, b, :, D:C], ALU.max, ALU.add).then_inc(signal_ready, 1)
                wait_slot(dve, scattered, t.back(RING), G)
                dve.wait_ge(const_made, CONST_MADE)
                V.tensor_copy(scatter_idx[:, t.j, :], run_idx[:, bass.ds(t.at(G), G)]).then_inc(sidx_staged, 1)
                V.tensor_copy(goes_now[:, t.j, :], goes_on[:, bass.ds(t.at(G), G)]).then_inc(goes_staged, 1)
                wait_turn(dve, gate_ready, t)
                wait_turn(dve, signal_ready, t)
                V.tensor_tensor(msg[:], signal[:], gate[:, b], ALU.mult).then_inc(msg_ready, 1)
                wait_turn(dve, run_kept, t.back(RING))
                wait_turn(dve, goes_staged, t)
                wait_turn(dve, msg_ready, t)
                for tile in range(G):
                    if tile:
                        before = run[:, t.j, tile - 1, :]
                        wait_turn(dve, run_step, t, G, G - tile)
                    else:
                        before = run[:, (t.j - 1) % RING, G - 1, :]
                        wait_turn(dve, run_step, t.back(1), G)
                    V.scalar_tensor_tensor(run[:, t.j, tile, :], before, goes_now[:, t.j, tile:tile + 1],
                                           msg[:, tile, :], ALU.mult, ALU.add).then_inc(run_step, 1)

            def turn2(t):
                if not t.is_number(TURNS - 1):
                    affine(t.back(-1))
                messages(t)

            affine(Turn(dve, 0, 0))
            run_turns(dve, turn2, TURNS, TURNS)

            def combine(s, n, values, index):
                V.tensor_copy(key[:], index).then_inc(s["key"], 1)
                V.tensor_copy(part[:], values).then_inc(s["part"], 1)
                dve.wait_ge(s["key"], n)
                V.tensor_copy(keys[:], key[:].to_broadcast([P, P])).then_inc(s["keys"], 1)
                dve.wait_ge(s["turned"], n)
                V.tensor_scalar(equal[:], k_ps[:, 0:P], key[:], None, ALU.is_equal).then_inc(s["equal"], 1)
                dve.wait_ge(s["equal"], n)
                V.tensor_tensor(earlier[:], equal[:], lower[:], ALU.mult).then_inc(s["earlier"], 1)
                dve.wait_ge(s["earlier"], n)
                V.reduce_sum(repeats[:, 0:1], earlier[:], axis=AX_X).then_inc(s["counted"], 1)
                dve.wait_ge(s["counted"], n)
                V.tensor_scalar(repeats[:, 1:2], repeats[:, 0:1], 0.0, BIG, ALU.is_gt, ALU.mult).then_inc(
                    s["flagged"], 1)
                dve.wait_ge(s["flagged"], n)
                V.tensor_tensor(once_idx[:], repeats[:, 1:2], key[:], ALU.add).then_inc(s["idx"], 1)
                dve.wait_ge(s["summed"], n)
                V.tensor_copy(total[:], w_ps[:, 0:D]).then_inc(s["total"], 1)

            wait_turn(dve, run_kept, end)
            with dve.If(dve.value_load(unsorted[0:1, 0:1], min_val=0, max_val=E)):
                with dve.Fori(0, EDGE_COLS - 1) as t:
                    n = dve.snap(t + 1)
                    kept = (t // G) * (G * P) + (t % G) * D
                    combine(each, n, pre[:, bass.ds(kept, D)], dst_f[:, bass.ds(t, 1)])
                    dve.wait_ge(each["added"], dve.snap(16 * t + 16))
            combine(tail, 1, run[:, (TURNS - 1) % RING, G - 1, :], dst_f[:, EDGE_COLS - 1:EDGE_COLS])


_INS = ["x", "src", "dst", "edge_attr_64", "L0_gnn_W_filter", "L0_gnn_b_filter", "L0_gnn_gamma_filter",
        "L0_gnn_beta_filter", "L0_gnn_W_core", "L0_gnn_b_core", "L0_gnn_gamma_core", "L0_gnn_beta_core"]


def kernel(**inputs):
    import numpy as np
    import concourse.bacc as bacc
    from concourse.bass_utils import run_bass_kernel_spmd

    nc = bacc.Bacc("TRN2", target_bir_lowering=False, num_devices=1)
    arrays, args = {}, []
    for name in _INS:
        a = np.ascontiguousarray(inputs[name])
        arrays[f"in_{name}"] = a
        args.append(nc.dram_tensor(f"in_{name}", a.shape, mybir.dt.from_np(a.dtype), kind="ExternalInput").ap())
    out = nc.dram_tensor("out", arrays["in_x"].shape, F32, kind="ExternalOutput").ap()
    gnn_layer(nc, *args, out)
    r = run_bass_kernel_spmd(nc, [arrays], core_ids=[0])
    return r.results[0]["out"]
```

```python
from contextlib import ExitStack

import concourse.bass as bass
from concourse import mybir

F32 = mybir.dt.float32
I32 = mybir.dt.int32
ALU = mybir.AluOpType
ACT = mybir.ActivationFunctionType
AX_X = mybir.AxisListType.X
P = 128
RING = 4
BIG = float(1 << 20)
EPS = 1e-5


class Turn:

    def __init__(self, eng, i, j, shift=0, known=None):
        self.eng, self.i, self.j, self.shift, self.known = eng, i, j, shift, {} if known is None else known
        if isinstance(i, int):
            self.i, self.j, self.shift = i + shift + j // RING, j % RING, 0

    def back(self, n):
        at = self.j - n
        return Turn(self.eng, self.i, at % RING, self.shift + at // RING, self.known)

    def within(self, turns):
        return not isinstance(self.i, int) or 0 <= RING * self.i + self.j < turns

    def exists(self):
        return not isinstance(self.i, int) or self.i >= 0

    def is_number(self, k):
        return isinstance(self.i, int) and RING * self.i + self.j == k

    def linear(self, scale, add):
        if isinstance(self.i, int):
            return scale * self.i + add
        if (scale, add) not in self.known:
            self.known[scale, add] = self.eng.snap(self.i * scale + add)
        return self.known[scale, add]

    def count(self, unit):
        return self.linear(unit, unit * (self.shift + 1))

    def count_all(self, unit, short=0):
        return self.linear(unit * RING, unit * (RING * self.shift + self.j + 1) - short)

    def at(self, step):
        return self.linear(step * RING, step * (RING * self.shift + self.j))


def wait_turn(eng, semaphore, turn, unit=1, short=0):
    if turn.exists():
        eng.wait_ge(semaphore, turn.count_all(unit, short))


def wait_slot(eng, semaphores, turn, count):
    if turn.exists():
        eng.wait_ge(semaphores[turn.j], turn.count(16 * count))


def run_turns(eng, body, looped, turns):
    for j in range(RING):
        body(Turn(eng, 0, j))
    with eng.Fori(1, looped // RING) as i:
        known = {}
        for j in range(RING):
            body(Turn(eng, i, j, known=known))
    for k in range(looped // RING * RING, turns):
        body(Turn(eng, k // RING, k % RING))


def gnn_layer(nc, x, src, dst, edge_attr, w_filter, b_filter, g_filter, be_filter,
              w_core, b_core, g_core, be_core, out):
    N, D = x.shape
    E = edge_attr.shape[0]
    G = 4
    C = 2 * D
    EDGE_COLS = -(-E // P)
    TURNS = EDGE_COLS // G
    DUP = P * EDGE_COLS - E
    NODE_ROWS = N // P
    REST = N - P * NODE_ROWS
    R = -(-NODE_ROWS // (TURNS - 3))
    NODE_TURNS = -(-NODE_ROWS // R)
    R_LAST = NODE_ROWS - R * (NODE_TURNS - 1)
    assert D == 64 and C == P and EDGE_COLS % G == 0 and TURNS % RING == 1 and DUP < EDGE_COLS
    assert 0 < REST <= P
    PA = (P - 1) // 16 * 16
    CHUNKS = TURNS + 1

    x_rows = x[0:P * NODE_ROWS, :].rearrange("(p r) d -> p r d", p=P)
    out_rows = out[0:P * NODE_ROWS, :].rearrange("(p r) d -> p r d", p=P)
    edge_rows = edge_attr[0:(P - 1) * EDGE_COLS, :].rearrange("(p t) d -> p t d", p=P - 1)
    edge_last = edge_attr[E - EDGE_COLS:E, :].rearrange("(p t) d -> p t d", p=1)

    ctx = ExitStack()
    with ctx:
        def sb(name, shape, dt=F32):
            return ctx.enter_context(nc.sbuf_tensor(name, shape, dt))

        def sem(name):
            return ctx.enter_context(nc.semaphore(name))

        def sems(name):
            return [sem(f"{name}{j}") for j in range(RING)]

        ident = sb("ident", [P, P])
        lower = sb("lower", [P, P])
        ones = sb("ones", [P, P])
        w_cat = sb("w_cat", [P, 2 * D])
        w_edge = sb("w_edge", [P, D])
        wt_nodes = sb("wt_nodes", [P, C])
        wt_edge = sb("wt_edge", [D, C])
        bias = sb("bias", [P, 1])
        gamma = sb("gamma", [P, 1])
        beta = sb("beta", [P, 1])
        eps = sb("eps", [P, 1])
        idx = sb("idx", [P, 2, EDGE_COLS + RING * G], I32)
        gather_idx = sb("gather_idx", [P, RING, 2, G], I32)
        dst_once = sb("dst_once", [P, EDGE_COLS], I32)
        dst_next = sb("dst_next", [P, EDGE_COLS], I32)
        same = sb("same", [P, EDGE_COLS])
        falls = sb("falls", [P, EDGE_COLS])
        dst_f = sb("dst_f", [P, EDGE_COLS])
        goes_now = sb("goes_now", [P, RING, G])
        run_idx = sb("run_idx", [P, EDGE_COLS], I32)
        goes_on = sb("goes_on", [P, EDGE_COLS])
        nfalls = sb("nfalls", [P, 1])
        is_sorted = sb("is_sorted", [P, 1])
        unsorted = sb("unsorted", [P, 1], I32)
        pre = sb("pre", [P, TURNS * G * P])
        nodes = sb("nodes", [P, RING, R, D])
        node_y = sb("node_y", [P, RING, R, D])
        node_sq = sb("node_sq", [P, R, D])
        node_sum = sb("node_sum", [P, R])
        node_var = sb("node_var", [P, 2, R])
        node_ln = sb("node_ln", [P, R])
        node_v = sb("node_v", [P, 2, R])
        node_root = sb("node_root", [P, 2, R])
        newton = sb("newton", [P, 2, R])
        node_rstd = sb("node_rstd", [P, R])
        ends = sb("ends", [P, RING, G, 2, D])
        edge = sb("edge", [P, RING, G, D])
        mean_of = sb("mean_of", [P, P])
        centre_of = sb("centre_of", [P, P])
        ends_t = sb("ends_t", [P, 2, G * P])
        edge_t = sb("edge_t", [D, RING, G * P])
        ends_sq = sb("ends_sq", [P, G * P])
        ends_ln = sb("ends_ln", [P, G * P])
        ends_rstd = sb("ends_rstd", [P, 2, G * P])
        ends_h = sb("ends_h", [P, 2, G * P])
        stats = sb("stats", [P, CHUNKS, 6])
        rest = sb("rest", [P, 6, D])
        rest_c = sb("rest_c", [P, 8])
        moments = sb("moments", [P, 2])
        bn = sb("bn", [P, 8])
        bn_root, root_gamma, neg_mean, bn_scale, bn_shift = (bn[:, k:k + 1] for k in (1, 4, 5, 6, 7))
        an = ends_t
        logs = ends_rstd[:].rearrange("p b (t c) -> p b t c", t=G)
        exps = ends_sq[:].rearrange("p (t c) -> p t c", t=G)
        spare = ends_h[:].rearrange("p b (t n d) -> p n b t d", t=G, n=2)
        gate = spare[:, 0]
        c_abs = spare[:, 1, 0]
        signal = sb("signal", [P, G, D])
        msg = sb("msg", [P, G, D])
        run = sb("run", [P, RING, G, D])
        scatter_idx = sb("scatter_idx", [P, RING, G], I32)
        key = sb("key", [P, 1])
        keys = sb("keys", [P, P])
        equal = sb("equal", [P, P])
        earlier = sb("earlier", [P, P])
        repeats = sb("repeats", [P, 2])
        once_idx = sb("once_idx", [P, 1], I32)
        part = sb("part", [P, D])
        total = sb("total", [P, D])

        def banks(name, shape):
            return [ctx.enter_context(nc.psum_tensor(f"{name}{b}", shape, F32)) for b in range(2)]

        turned_ps = banks("turned_ps", [P, G * P])
        centred_ps = banks("centred_ps", [P, G * P])
        pre_ps = banks("pre_ps", [P, G * P])
        edge_ps = ctx.enter_context(nc.psum_tensor("edge_ps", [P, G * P], F32))
        var_ps = ctx.enter_context(nc.psum_tensor("var_ps", [P, G * P], F32))
        w_ps, k_ps = centred_ps

        idx_loaded = sem("idx_loaded")
        const_loaded = sem("const_loaded")
        const_made = sem("const_made")
        waited = sem("waited")
        pe_waited = sem("pe_waited")
        act_waited = sem("act_waited")
        mean_cleared = sem("mean_cleared")
        pads_set = sem("pads_set")
        w_turned = sem("w_turned")
        w_ready = sem("w_ready")
        rest_loaded = sem("rest_loaded")
        rest_stored = sem("rest_stored")
        rest_var = sem("rest_var")
        rest_ready = sem("rest_ready")
        rest_ln = sem("rest_ln")
        rest_rstd = sem("rest_rstd")
        link = sem("link")
        bn_ready = sem("bn_ready")
        falls_ready = sem("falls_ready")
        falls_summed = sem("falls_summed")
        runs_ready = sem("runs_ready")
        idx_staged = sem("idx_staged")
        gathered = sems("gathered")
        nodes_loaded = sems("nodes_loaded")
        edges_loaded = sems("edges_loaded")
        node_summed = sem("node_summed")
        node_centred = sem("node_centred")
        node_squared = sem("node_squared")
        node_var_ready = sem("node_var_ready")
        node_ln_ready = sem("node_ln_ready")
        node_root_ready = sem("node_root_ready")
        newton_1 = sem("newton_1")
        newton_2 = sem("newton_2")
        node_rstd_ready = sem("node_rstd_ready")
        node_h_ready = sem("node_h_ready")
        y_ready = sem("y_ready")
        y_stored = sems("y_stored")
        centre_ready = sem("centre_ready")
        edge_turned = sem("edge_turned")
        turned = sem("turned")
        ends_copied = sem("ends_copied")
        edge_copied = sem("edge_copied")
        centred = sem("centred")
        squared = sem("squared")
        var_done = sem("var_done")
        ln_ready = sem("ln_ready")
        rstd_ready = sem("rstd_ready")
        h_ready = sem("h_ready")
        multiplied = sem("multiplied")
        pre_copied = sem("pre_copied")
        counted = sem("counted")
        bn_var = sem("bn_var")
        bn_ln = sem("bn_ln")
        bn_rstd = sem("bn_rstd")
        affine_done = sem("affine_done")
        act_turned = sem("act_turned")
        gate_exp = sem("gate_exp")
        abs_done = sem("abs_done")
        core_exp = sem("core_exp")
        log_done = sem("log_done")
        gate_ready = sem("gate_ready")
        signal_ready = sem("signal_ready")
        msg_ready = sem("msg_ready")
        run_step = sem("run_step")
        sidx_staged = sem("sidx_staged")
        goes_staged = sem("goes_staged")
        scattered = sems("scattered")
        run_kept = sem("run_kept")
        def combine_sems(name):
            return {s: sem(f"{name}_{s}") for s in
                    ("key", "keys", "turned", "equal", "earlier", "counted", "flagged", "idx", "part", "summed",
                     "total", "added")}
        tail = combine_sems("tail")
        each = combine_sems("each")

        block = ctx.enter_context(nc.Block())
        LOOPED = NODE_TURNS - 1
        LATE = TURNS - 2
        CONST_LOADED = 16 * (4 + 6 + 6)
        IDX_LOADED = 16 * 6
        CONST_MADE = 9

        @block.sync
        def _(sp):
            for k, table in enumerate((dst, src)):
                rows = table[0:(P - 1) * EDGE_COLS].rearrange("(p t) -> p t", p=P - 1)
                sp.dma_start(idx[0:PA, k, 0:EDGE_COLS], rows[0:PA, :]).then_inc(idx_loaded, 16)
                sp.dma_start(idx[PA:P - 1, k, 0:EDGE_COLS], rows[PA:P - 1, :]).then_inc(idx_loaded, 16)
                sp.dma_start(idx[P - 1:P, k, 0:EDGE_COLS],
                             table[E - EDGE_COLS:E].rearrange("(p t) -> p t", p=1)).then_inc(idx_loaded, 16)

            def loads(t):
                if t.within(NODE_TURNS):
                    rows = R_LAST if t.is_number(NODE_TURNS - 1) else R
                    wait_turn(sp, y_ready, t.back(RING))
                    sp.dma_start(nodes[:, t.j, 0:rows, :], x_rows[:, bass.ds(t.at(R), rows), :]).then_inc(
                        nodes_loaded[t.j], 16)
                if t.within(TURNS):
                    wait_turn(sp, edge_turned, t.back(RING))
                    for d, s in ((edge[0:PA], edge_rows[0:PA]), (edge[PA:P - 1], edge_rows[PA:P - 1]),
                                 (edge[P - 1:P], edge_last)):
                        sp.dma_start(d[:, t.j, :, :], s[:, bass.ds(t.at(G), G), :]).then_inc(edges_loaded[t.j], 16)

            def store(t):
                if not t.within(NODE_TURNS):
                    return
                rows = R_LAST if t.is_number(NODE_TURNS - 1) else R
                wait_turn(sp, y_ready, t)
                sp.dma_start(out_rows[:, bass.ds(t.at(R), rows), :], node_y[:, t.j, 0:rows, :]).then_inc(
                    y_stored[t.j], 16)

            def turn(t):
                store(t.back(RING))
                loads(t)
                if t.is_number(1):
                    small_loads()

            def small_loads():
                sp.dma_start(rest[0:REST, 0, :], x[P * NODE_ROWS:N, :]).then_inc(rest_loaded, 16)
                for w, at in ((w_filter, 0), (w_core, D)):
                    sp.dma_start(w_cat[at:at + D, :], w[:, 0:2 * D]).then_inc(const_loaded, 16)
                    sp.dma_start(w_edge[at:at + D, :], w[:, 2 * D:3 * D]).then_inc(const_loaded, 16)
                for col, filt, core in ((bias, b_filter, b_core), (gamma, g_filter, g_core),
                                        (beta, be_filter, be_core)):
                    for v, at in ((filt, 0), (core, D)):
                        sp.dma_start(col[at:at + D, :], v.rearrange("(d o) -> d o", o=1)).then_inc(const_loaded, 16)
                sp.wait_ge(pads_set, 3)
                rows = dst[0:(P - 1) * EDGE_COLS].rearrange("(p t) -> p t", p=P - 1)
                after = dst[1:(P - 1) * EDGE_COLS + 1].rearrange("(p t) -> p t", p=P - 1)
                for d, s in ((dst_once, rows), (dst_next, after)):
                    sp.dma_start(d[0:PA, :], s[0:PA, :]).then_inc(const_loaded, 16)
                    sp.dma_start(d[PA:P - 1, :], s[PA:P - 1, :]).then_inc(const_loaded, 16)
                sp.dma_start(dst_once[P - 1:P, DUP:EDGE_COLS],
                             dst[E - EDGE_COLS + DUP:E].rearrange("(p t) -> p t", p=1)).then_inc(const_loaded, 16)
                sp.dma_start(dst_next[P - 1:P, 0:EDGE_COLS - 1],
                             dst[E - EDGE_COLS + 1:E].rearrange("(p t) -> p t", p=1)).then_inc(const_loaded, 16)

            run_turns(sp, turn, LOOPED, TURNS + RING)
            sp.wait_ge(rest_ready, 1)
            sp.dma_start(out[P * NODE_ROWS:N, :], rest[0:REST, 5, :]).then_inc(rest_stored, 16)


        @block.gpsimd
        def _(pool):
            nc.gpsimd.memset(idx[:, :, EDGE_COLS:], 0).then_inc(pads_set, 1)
            nc.gpsimd.memset(dst_once[:], int(BIG)).then_inc(pads_set, 1)
            nc.gpsimd.memset(dst_next[:], int(BIG)).then_inc(pads_set, 1)
            nc.gpsimd.memset(ident[:], 0.0).then_inc(const_made, 1)
            nc.gpsimd.memset(ones[:], 1.0).then_inc(const_made, 1)
            nc.gpsimd.memset(eps[:], EPS).then_inc(const_made, 1)
            nc.gpsimd.memset(goes_on[:, 0:1], 0.0).then_inc(const_made, 1)
            nc.gpsimd.memset(run[:, RING - 1, G - 1, :], 0.0).then_inc(const_made, 1)
            nc.gpsimd.memset(mean_of[:], 0.0).then_inc(mean_cleared, 1)
            pool.wait_ge(mean_cleared, 1)
            for half in range(2):
                part_of = slice(half * D, (half + 1) * D)
                nc.gpsimd.memset(mean_of[part_of, part_of], 1.0 / D).then_inc(const_made, 1)
            pool.wait_ge(const_made, 7)
            nc.gpsimd.affine_select(out=ident[:], in_=ident[:], compare_op=ALU.not_equal, fill=1.0, base=0,
                                    pattern=[[-1, P]], channel_multiplier=1).then_inc(const_made, 1)
            nc.gpsimd.affine_select(out=lower[:], in_=ones[:], compare_op=ALU.is_gt, fill=0.0, base=0,
                                    pattern=[[-1, P]], channel_multiplier=1).then_inc(const_made, 1)

            def gathers(t):
                wait_turn(pool, turned, t.back(RING))
                wait_turn(pool, idx_staged, t)
                pool.sem_inc(waited, 1)
                for tile in range(G):
                    for side in range(2):
                        pool.indirect_dma_start(
                            out=ends[:, t.j, tile, side, :], out_offset=None, in_=x,
                            in_offset=bass.IndirectOffsetOnAxis(ap=gather_idx[:, t.j, side, tile:tile + 1], axis=0),
                        ).then_inc(gathered[t.j], 16)

            run_turns(pool, gathers, TURNS, TURNS)

            end = Turn(pool, TURNS // RING, 0)
            for n in range(RING):
                wait_slot(pool, y_stored, Turn(pool, 0, NODE_TURNS - 1).back(n), 1)
            pool.wait_ge(rest_stored, 16)

            last_row = pool.snap(pool.to_reg(N - 1))

            def add_rows(values, index):
                return pool.indirect_dma_start(
                    out=out, out_offset=bass.IndirectOffsetOnAxis(ap=index, axis=0), in_=values, in_offset=None,
                    bounds_check=last_row, oob_is_err=False, compute_op=ALU.add)

            def scatter(t):
                wait_turn(pool, sidx_staged, t)
                for tile in range(G):
                    if t.is_number(TURNS - 1) and tile == G - 1:
                        continue
                    wait_turn(pool, run_step, t, G, G - 1 - tile)
                    pool.sem_inc(waited, 1)
                    add_rows(run[:, t.j, tile, :], scatter_idx[:, t.j, tile:tile + 1]).then_inc(scattered[t.j], 16)

            run_turns(pool, scatter, TURNS, TURNS)
            for n in range(1, RING):
                wait_slot(pool, scattered, end.back(n), G)
            pool.wait_ge(scattered[end.j], end.count(16 * G) - 16)

            with pool.If(pool.value_load(unsorted[0:1, 0:1], min_val=0, max_val=E)):
                with pool.Fori(0, EDGE_COLS - 1) as t:
                    pool.wait_ge(each["total"], pool.snap(t + 1))
                    pool.wait_ge(each["idx"], pool.snap(t + 1))
                    pool.sem_inc(waited, 1)
                    add_rows(total[:], once_idx[:]).then_inc(each["added"], 16)
                    pool.wait_ge(each["added"], pool.snap(16 * t + 16))
            pool.wait_ge(tail["total"], 1)
            pool.wait_ge(tail["idx"], 1)
            add_rows(total[:], once_idx[:]).then_inc(tail["added"], 16)
            pool.wait_ge(tail["added"], 16)

        @block.scalar
        def _(act):
            def stage_idx(t):
                nc.scalar.copy(gather_idx[:, t.j, :, :], idx[:, :, bass.ds(t.at(G), G)]).then_inc(idx_staged, 1)

            nc.scalar.preload_act_table_set("natural_log_exp_and_others")
            act.wait_ge(idx_loaded, IDX_LOADED)
            act.wait_ge(pads_set, 3)
            for j in range(RING):
                stage_idx(Turn(act, 0, j))
            act.wait_ge(w_turned, 1)
            nc.scalar.copy(wt_nodes[:], w_ps[:, 0:C]).then_inc(w_ready, 1)
            nc.scalar.copy(wt_edge[:], w_ps[0:D, C:2 * C]).then_inc(w_ready, 1)

            act.wait_ge(rest_var, 1)
            act.wait_ge(const_made, CONST_MADE)
            nc.scalar.activation(rest_c[0:REST, 3:4], rest_c[0:REST, 2:3], ACT.Ln, bias=eps[0:REST, :],
                                 scale=1.0 / D).then_inc(rest_ln, 1)
            act.wait_ge(rest_ln, 1)
            nc.scalar.activation(rest_c[0:REST, 4:5], rest_c[0:REST, 3:4], ACT.Exp, scale=-0.5).then_inc(rest_rstd, 1)

            def copy_turned(t):
                if not t.within(TURNS):
                    return
                wait_turn(act, multiplied, t.back(RING))
                wait_turn(act, edge_turned, t)
                nc.scalar.copy(edge_t[:, t.j, :], edge_ps[0:D, :]).then_inc(edge_copied, 1)
                wait_turn(act, centred, t.back(2))
                wait_turn(act, turned, t)
                nc.scalar.copy(ends_t[:, t.j % 2, :], turned_ps[t.j % 2][:]).then_inc(ends_copied, 1)
                if not t.is_number(TURNS - 1):
                    stage_idx(t.back(-RING))

            def root_ends(t):
                if not t.within(TURNS):
                    return
                wait_turn(act, h_ready, t.back(2))
                wait_turn(act, var_done, t)
                nc.scalar.activation(ends_ln[:], var_ps[:], ACT.Ln, bias=eps[:], scale=1.0).then_inc(ln_ready, 1)
                wait_turn(act, ln_ready, t)
                nc.scalar.activation(ends_rstd[:, t.j % 2, :], ends_ln[:], ACT.Exp, scale=-0.5).then_inc(
                    rstd_ready, 1)

            def keep_pre(t):
                if not t.within(TURNS):
                    return
                wait_turn(act, multiplied, t)
                act.wait_ge(const_loaded, CONST_LOADED)
                nc.scalar.activation(pre[:, bass.ds(t.at(G * P), G * P)], pre_ps[t.j % 2][:], ACT.Identity,
                                     bias=bias[:], scale=1.0).then_inc(pre_copied, 1)

            def square_nodes(t):
                if not t.within(NODE_TURNS):
                    return
                wait_turn(act, node_var_ready, t.back(1))
                wait_turn(act, node_centred, t)
                nc.scalar.activation(node_sq[:], node_y[:, t.j], ACT.Square).then_inc(node_squared, 1)

            def square_ends(t):
                if not t.within(TURNS):
                    return
                wait_turn(act, var_done, t.back(1))
                wait_turn(act, centred, t)
                nc.scalar.activation(ends_sq[:], centred_ps[t.j % 2][:], ACT.Square).then_inc(squared, 1)

            def root_nodes(t):
                if not t.within(NODE_TURNS):
                    return
                b = t.j % 2
                wait_turn(act, node_h_ready, t.back(2))
                wait_turn(act, node_var_ready, t)
                nc.scalar.activation(node_ln[:], node_var[:, b, :], ACT.Ln, bias=eps[:], scale=1.0 / D).then_inc(
                    node_ln_ready, 1)
                nc.scalar.activation(node_v[:, b, :], node_var[:, b, :], ACT.Identity, bias=eps[:], scale=1.0 / D)
                wait_turn(act, node_ln_ready, t)
                nc.scalar.activation(node_root[:, b, :], node_ln[:], ACT.Exp, scale=-0.5).then_inc(
                    node_root_ready, 1)

            def turn(t):
                copy_turned(t)
                root_ends(t.back(1))
                keep_pre(t.back(2))
                square_nodes(t)
                square_ends(t)
                root_nodes(t)

            run_turns(act, turn, LOOPED, LATE)
            late, last = Turn(act, 0, LATE), Turn(act, 0, LATE + 1)
            root_ends(late.back(1))
            keep_pre(late.back(2))
            keep_pre(late.back(1))
            copy_turned(late)
            square_ends(late)
            root_ends(late)
            copy_turned(last)
            keep_pre(late)
            square_ends(last)
            root_ends(last)
            keep_pre(last)

            act.wait_ge(bn_var, 1)
            nc.scalar.activation(bn[:, 0:1], moments[:, 1:2], ACT.Ln, bias=eps[:], scale=1.0).then_inc(bn_ln, 1)
            act.wait_ge(bn_ln, 1)
            nc.scalar.activation(bn_root, bn[:, 0:1], ACT.Exp, scale=-0.5).then_inc(bn_rstd, 1)

            def keep_runs(t):
                if not t.exists():
                    return
                wait_turn(act, run_step, t, G)
                act.sem_inc(act_waited, 1)
                nc.scalar.copy(pre[:, bass.ds(t.at(G * P), G * D)],
                               run[:, t.j, :, :].rearrange("p t d -> p (t d)")).then_inc(run_kept, 1)

            def affine(t):
                wait_turn(act, act_turned, t.back(2))
                nc.scalar.activation(an[:, t.j % 2, :], pre[:, bass.ds(t.at(G * P), G * P)], ACT.Identity,
                                     bias=bn_shift, scale=bn_scale).then_inc(affine_done, 1)

            def exponentials(t):
                b = t.j % 2
                edges = turned_ps[b][:].rearrange("p (t c) -> p t c", t=G)
                wait_turn(act, act_turned, t)
                nc.scalar.activation(c_abs, edges[:, :, D:C], ACT.Abs).then_inc(abs_done, 1)
                wait_turn(act, log_done, t.back(1))
                nc.scalar.activation(exps[:, :, 0:D], edges[:, :, 0:D], ACT.Exp).then_inc(gate_exp, 1)
                wait_turn(act, abs_done, t)
                nc.scalar.activation(exps[:, :, D:C], c_abs, ACT.Exp, scale=-1.0).then_inc(core_exp, 1)
                if not t.is_number(0) and not t.is_number(TURNS - 1):
                    affine(t.back(-1))
                wait_turn(act, gate_exp, t)
                wait_turn(act, core_exp, t)
                wait_turn(act, signal_ready, t.back(2))
                nc.scalar.activation(logs[:, b], exps[:], ACT.Ln, bias=ones[:, 0:1], scale=1.0).then_inc(log_done, 1)
                wait_turn(act, log_done, t)
                wait_turn(act, msg_ready, t.back(2))
                nc.scalar.activation(gate[:, b], logs[:, b, :, 0:D], ACT.Exp, scale=-1.0).then_inc(gate_ready, 1)
                keep_runs(t.back(1))

            act.wait_ge(bn_ready, 1)
            run_turns(act, exponentials, TURNS, TURNS)
            keep_runs(last)

        @block.tensor
        def _(pe):
            def combine(s, n):
                pe.wait_ge(s["keys"], n)
                nc.tensor.transpose(k_ps[:, 0:P], keys[:], ident[:]).then_inc(s["turned"], 1)
                pe.wait_ge(s["equal"], n)
                pe.wait_ge(s["part"], n)
                nc.tensor.matmul(w_ps[:, 0:D], equal[:], part[:], start=True, stop=True).then_inc(s["summed"], 1)

            pe.wait_ge(const_made, CONST_MADE)
            pe.wait_ge(const_loaded, CONST_LOADED)
            nc.tensor.transpose(w_ps[:, 0:C], w_cat[:], ident[:])
            nc.tensor.transpose(w_ps[0:D, C:2 * C], w_edge[:], ident[:]).then_inc(w_turned, 1)
            pe.wait_ge(falls_ready, 1)
            nc.tensor.matmul(k_ps[:, 0:1], ones[:], nfalls[:], start=True, stop=True).then_inc(falls_summed, 1)
            pe.wait_ge(w_ready, 2)

            pe.wait_ge(centre_ready, 1)

            def turn_rows(t):
                if not t.within(TURNS):
                    return
                b = t.j % 2
                wait_turn(pe, edge_copied, t.back(1))
                wait_slot(pe, edges_loaded, t, 3)
                pe.sem_inc(pe_waited, 1)
                for tile in range(G):
                    last = nc.tensor.transpose(edge_ps[0:D, tile * P:(tile + 1) * P], edge[:, t.j, tile, :],
                                               ident[:])
                last.then_inc(edge_turned, 1)
                wait_turn(pe, ends_copied, t.back(2))
                wait_slot(pe, gathered, t, 2 * G)
                for tile in range(G):
                    last = nc.tensor.transpose(turned_ps[b][:, tile * P:(tile + 1) * P],
                                               ends[:, t.j, tile].rearrange("p s d -> p (s d)"), ident[:])
                last.then_inc(turned, 1)

            def centre(t):
                if not t.within(TURNS):
                    return
                wait_turn(pe, h_ready, t.back(2))
                wait_turn(pe, ends_copied, t)
                nc.tensor.matmul(centred_ps[t.j % 2][:], centre_of[:], ends_t[:, t.j % 2, :], start=True,
                                 stop=True).then_inc(centred, 1)

            def variance(t):
                if not t.within(TURNS):
                    return
                wait_turn(pe, ln_ready, t.back(1))
                wait_turn(pe, squared, t)
                nc.tensor.matmul(var_ps[:], mean_of[:], ends_sq[:], start=True, stop=True).then_inc(var_done, 1)

            def product(t):
                if not t.within(TURNS):
                    return
                b = t.j % 2
                wait_turn(pe, pre_copied, t.back(2))
                wait_turn(pe, edge_copied, t)
                nc.tensor.matmul(pre_ps[b][:], wt_edge[:], edge_t[:, t.j, :], start=True, stop=False)
                wait_turn(pe, h_ready, t)
                nc.tensor.matmul(pre_ps[b][:], wt_nodes[:], ends_h[:, b, :], start=False, stop=True).then_inc(
                    multiplied, 1)

            def turn(t):
                turn_rows(t)
                variance(t.back(1))
                product(t.back(2))
                centre(t)

            run_turns(pe, turn, LOOPED, LATE)
            late, last = Turn(pe, 0, LATE), Turn(pe, 0, LATE + 1)
            variance(late.back(1))
            product(late.back(2))
            product(late.back(1))
            turn_rows(late)
            centre(late)
            variance(late)
            turn_rows(last)
            product(late)
            centre(last)
            variance(last)
            product(last)

            def turn_activations(t):
                b = t.j % 2
                wait_turn(pe, signal_ready, t.back(2))
                wait_turn(pe, affine_done, t)
                pe.wait_ge(const_made, CONST_MADE)
                for tile in range(G):
                    at = slice(tile * P, (tile + 1) * P)
                    last = nc.tensor.transpose(turned_ps[b][:, at], an[:, b, at], ident[:])
                last.then_inc(act_turned, 1)

            run_turns(pe, turn_activations, TURNS, TURNS)

            pe.wait_ge(runs_ready, 1)
            with pe.If(pe.value_load(unsorted[0:1, 0:1], min_val=0, max_val=E)):
                with pe.Fori(0, EDGE_COLS - 1) as t:
                    combine(each, pe.snap(t + 1))
            combine(tail, 1)

        @block.vector
        def _(dve):
            links = [0]

            def linked(instruction):
                links[0] += 1
                instruction.then_inc(link, 1)
                dve.wait_ge(link, links[0])

            V = nc.vector

            def per_row(col):
                return col.unsqueeze(2).to_broadcast([P, R, D])

            dve.wait_ge(const_loaded, CONST_LOADED)
            dve.wait_ge(idx_loaded, IDX_LOADED)
            dve.wait_ge(const_made, CONST_MADE)
            V.tensor_tensor(centre_of[:], ident[:], mean_of[:], ALU.subtract).then_inc(centre_ready, 1)
            linked(V.tensor_tensor(falls[:], dst_next[:], idx[:, 0, 0:EDGE_COLS], ALU.is_lt))
            V.reduce_sum(nfalls[:], falls[:], axis=AX_X).then_inc(falls_ready, 1)
            linked(V.tensor_tensor(same[:], dst_next[:], dst_once[:], ALU.is_equal))
            linked(V.tensor_copy(dst_f[:], dst_once[:]))
            dve.wait_ge(falls_summed, 1)
            linked(V.tensor_scalar(is_sorted[:], k_ps[:, 0:1], 0.0, None, ALU.is_equal))
            linked(V.tensor_copy(unsorted[:], k_ps[:, 0:1]))
            linked(V.tensor_scalar(goes_on[:, 1:EDGE_COLS], same[:, 0:EDGE_COLS - 1], is_sorted[:], None, ALU.mult))
            linked(V.tensor_scalar(falls[:], same[:], -1.0, 1.0, ALU.mult, ALU.add))
            linked(V.tensor_scalar(same[:], falls[:], is_sorted[:], -BIG, ALU.mult, ALU.mult))
            V.scalar_tensor_tensor(run_idx[:], same[:], BIG, dst_f[:], ALU.add, ALU.add).then_inc(runs_ready, 1)

            r = slice(0, REST)
            dve.wait_ge(rest_loaded, 16)
            linked(V.reduce_sum(rest_c[r, 0:1], rest[r, 0, :], axis=AX_X))
            linked(V.tensor_scalar(rest_c[r, 1:2], rest_c[r, 0:1], 1.0 / D, None, ALU.mult))
            linked(V.tensor_scalar(rest[r, 1, :], rest[r, 0, :], rest_c[r, 1:2], None, ALU.subtract))
            linked(V.tensor_tensor(rest[r, 2, :], rest[r, 1, :], rest[r, 1, :], ALU.mult))
            V.reduce_sum(rest_c[r, 2:3], rest[r, 2, :], axis=AX_X).then_inc(rest_var, 1)
            dve.wait_ge(rest_rstd, 1)
            v, root = rest_c[r, 5:6], rest_c[r, 4:5]
            linked(V.tensor_scalar(v, rest_c[r, 2:3], 1.0 / D, EPS, ALU.mult, ALU.add))
            linked(V.tensor_scalar(rest_c[r, 6:7], v, root, root, ALU.mult, ALU.mult))
            linked(V.tensor_scalar(rest_c[r, 6:7], rest_c[r, 6:7], -0.5, 1.5, ALU.mult, ALU.add))
            linked(V.tensor_scalar(rest_c[r, 7:8], rest_c[r, 6:7], root, None, ALU.mult))
            linked(V.tensor_scalar(rest[r, 3, :], rest[r, 1, :], 0.0, rest_c[r, 7:8], ALU.max, ALU.mult))
            V.tensor_tensor(rest[r, 5, :], rest[r, 3, :], rest[r, 0, :], ALU.add).then_inc(rest_ready, 1)

            linked(V.tensor_scalar(gamma[0:D, :], gamma[0:D, :], -1.0, None, ALU.mult))
            linked(V.tensor_scalar(beta[0:D, :], beta[0:D, :], -1.0, None, ALU.mult))

            def sum_nodes(t):
                if not t.within(NODE_TURNS):
                    return
                wait_slot(dve, nodes_loaded, t, 1)
                V.reduce_sum(node_sum[:], nodes[:, t.j], axis=AX_X).then_inc(node_summed, 1)

            def centre_nodes(t):
                if not t.within(NODE_TURNS):
                    return
                wait_slot(dve, y_stored, t.back(RING), 1)
                wait_turn(dve, node_summed, t)
                V.scalar_tensor_tensor(node_y[:, t.j], per_row(node_sum[:]), -1.0 / D, nodes[:, t.j], ALU.mult,
                                       ALU.add).then_inc(node_centred, 1)

            def variance_nodes(t):
                if not t.within(NODE_TURNS):
                    return
                wait_turn(dve, node_squared, t)
                V.reduce_sum(node_var[:, t.j % 2, :], node_sq[:], axis=AX_X).then_inc(node_var_ready, 1)

            def newton_nodes_1(t):
                if not t.within(NODE_TURNS):
                    return
                wait_turn(dve, node_root_ready, t)
                V.tensor_tensor(newton[:, 0, :], node_v[:, t.j % 2, :], node_root[:, t.j % 2, :], ALU.mult).then_inc(
                    newton_1, 1)

            def newton_nodes_2(t):
                if not t.within(NODE_TURNS):
                    return
                wait_turn(dve, newton_1, t)
                V.scalar_tensor_tensor(newton[:, 1, :], newton[:, 0, :], -0.5, node_root[:, t.j % 2, :], ALU.mult,
                                       ALU.mult).then_inc(newton_2, 1)

            def newton_nodes_3(t):
                if not t.within(NODE_TURNS):
                    return
                wait_turn(dve, newton_2, t)
                V.scalar_tensor_tensor(node_rstd[:], newton[:, 1, :], 1.5, node_root[:, t.j % 2, :], ALU.add,
                                       ALU.mult).then_inc(node_rstd_ready, 1)

            def h_nodes(t):
                if not t.within(NODE_TURNS):
                    return
                wait_turn(dve, node_rstd_ready, t)
                V.scalar_tensor_tensor(node_y[:, t.j], node_y[:, t.j], 0.0, per_row(node_rstd[:]), ALU.max,
                                       ALU.mult).then_inc(node_h_ready, 1)

            def add_nodes(t):
                if not t.within(NODE_TURNS):
                    return
                wait_turn(dve, node_h_ready, t)
                V.tensor_tensor(node_y[:, t.j], node_y[:, t.j], nodes[:, t.j], ALU.add).then_inc(y_ready, 1)

            def normalise_ends(t):
                if not t.within(TURNS):
                    return
                b = t.j % 2
                wait_turn(dve, multiplied, t.back(2))
                wait_turn(dve, rstd_ready, t)
                V.scalar_tensor_tensor(ends_h[:, b, :], centred_ps[b][:], 0.0, ends_rstd[:, b, :], ALU.max,
                                       ALU.mult).then_inc(h_ready, 1)

            def count_stats(t):
                if not t.within(TURNS):
                    return
                wait_turn(dve, pre_copied, t)
                dve.wait_ge(const_made, CONST_MADE)
                cols = pre[:, bass.ds(t.at(G * P), G * P)].rearrange("c (t p) -> c t p", t=G)
                V.bn_stats(stats[:, bass.ds(t.at(1), 1), :], cols[:, :, 0:P - 1]).then_inc(counted, 1)

            def turn(t):
                sum_nodes(t)
                centre_nodes(t)
                newton_nodes_1(t.back(1))
                normalise_ends(t.back(1))
                newton_nodes_2(t.back(1))
                count_stats(t.back(3))
                newton_nodes_3(t.back(1))
                h_nodes(t.back(1))
                variance_nodes(t)
                add_nodes(t.back(1))

            run_turns(dve, turn, LOOPED, LATE)
            late, last = Turn(dve, 0, LATE), Turn(dve, 0, LATE + 1)
            normalise_ends(late.back(1))
            for n in (3, 2, 1):
                count_stats(late.back(n))
            for t in (late, last):
                normalise_ends(t)
                count_stats(t)
            last_cols = pre[:].rearrange("c (t p) -> c t p", p=P)[:, DUP:EDGE_COLS, P - 1]
            linked(V.bn_stats(stats[:, TURNS, :], last_cols))
            wait_turn(dve, counted, last)
            V.bn_aggr(moments[:], stats[:]).then_inc(bn_var, 1)
            dve.wait_ge(bn_var, 1)
            linked(V.tensor_scalar(neg_mean, moments[:, 0:1], -1.0, None, ALU.mult))
            dve.wait_ge(bn_rstd, 1)
            V.tensor_tensor(root_gamma, bn_root, gamma[:], ALU.mult)
            linked(V.tensor_scalar(bn[:, 2:3], moments[:, 1:2], EPS, bn_root, ALU.add, ALU.mult))
            linked(V.tensor_scalar(bn[:, 3:4], bn[:, 2:3], bn_root, -0.5, ALU.mult, ALU.mult))
            linked(V.tensor_scalar(bn_scale, bn[:, 3:4], 1.5, root_gamma, ALU.add, ALU.mult))
            V.scalar_tensor_tensor(bn_shift, bn_scale, neg_mean, beta[:], ALU.mult, ALU.add).then_inc(bn_ready, 1)

            dve.wait_ge(bn_ready, 1)
            for k in range(2):
                V.tensor_scalar(an[:, k, :], pre[:, k * G * P:(k + 1) * G * P], bn_scale, bn_shift, ALU.mult,
                                ALU.add).then_inc(affine_done, 1)

            def messages(t):
                b = t.j % 2
                core = turned_ps[b][:].rearrange("p (t c) -> p t c", t=G)[:, :, D:C]
                wait_turn(dve, log_done, t)
                V.scalar_tensor_tensor(signal[:], core, 0.0, logs[:, b, :, D:C], ALU.max, ALU.add).then_inc(signal_ready, 1)
                wait_slot(dve, scattered, t.back(RING), G)
                dve.wait_ge(const_made, CONST_MADE)
                V.tensor_copy(scatter_idx[:, t.j, :], run_idx[:, bass.ds(t.at(G), G)]).then_inc(sidx_staged, 1)
                V.tensor_copy(goes_now[:, t.j, :], goes_on[:, bass.ds(t.at(G), G)]).then_inc(goes_staged, 1)
                wait_turn(dve, gate_ready, t)
                wait_turn(dve, signal_ready, t)
                V.tensor_tensor(msg[:], signal[:], gate[:, b], ALU.mult).then_inc(msg_ready, 1)
                wait_turn(dve, run_kept, t.back(RING))
                wait_turn(dve, goes_staged, t)
                wait_turn(dve, msg_ready, t)
                for tile in range(G):
                    if tile:
                        before = run[:, t.j, tile - 1, :]
                        wait_turn(dve, run_step, t, G, G - tile)
                    else:
                        before = run[:, (t.j - 1) % RING, G - 1, :]
                        wait_turn(dve, run_step, t.back(1), G)
                    V.scalar_tensor_tensor(run[:, t.j, tile, :], before, goes_now[:, t.j, tile:tile + 1],
                                           msg[:, tile, :], ALU.mult, ALU.add).then_inc(run_step, 1)

            run_turns(dve, messages, TURNS, TURNS)

            def combine(s, n, values, index):
                V.tensor_copy(key[:], index).then_inc(s["key"], 1)
                V.tensor_copy(part[:], values).then_inc(s["part"], 1)
                dve.wait_ge(s["key"], n)
                V.tensor_copy(keys[:], key[:].to_broadcast([P, P])).then_inc(s["keys"], 1)
                dve.wait_ge(s["turned"], n)
                V.tensor_scalar(equal[:], k_ps[:, 0:P], key[:], None, ALU.is_equal).then_inc(s["equal"], 1)
                dve.wait_ge(s["equal"], n)
                V.tensor_tensor(earlier[:], equal[:], lower[:], ALU.mult).then_inc(s["earlier"], 1)
                dve.wait_ge(s["earlier"], n)
                V.reduce_sum(repeats[:, 0:1], earlier[:], axis=AX_X).then_inc(s["counted"], 1)
                dve.wait_ge(s["counted"], n)
                V.tensor_scalar(repeats[:, 1:2], repeats[:, 0:1], 0.0, BIG, ALU.is_gt, ALU.mult).then_inc(
                    s["flagged"], 1)
                dve.wait_ge(s["flagged"], n)
                V.tensor_tensor(once_idx[:], repeats[:, 1:2], key[:], ALU.add).then_inc(s["idx"], 1)
                dve.wait_ge(s["summed"], n)
                V.tensor_copy(total[:], w_ps[:, 0:D]).then_inc(s["total"], 1)

            wait_turn(dve, run_kept, last)
            with dve.If(dve.value_load(unsorted[0:1, 0:1], min_val=0, max_val=E)):
                with dve.Fori(0, EDGE_COLS - 1) as t:
                    n = dve.snap(t + 1)
                    kept = (t // G) * (G * P) + (t % G) * D
                    combine(each, n, pre[:, bass.ds(kept, D)], dst_f[:, bass.ds(t, 1)])
                    dve.wait_ge(each["added"], dve.snap(16 * t + 16))
            combine(tail, 1, run[:, (TURNS - 1) % RING, G - 1, :], dst_f[:, EDGE_COLS - 1:EDGE_COLS])


_INS = ["x", "src", "dst", "edge_attr_64", "L0_gnn_W_filter", "L0_gnn_b_filter", "L0_gnn_gamma_filter",
        "L0_gnn_beta_filter", "L0_gnn_W_core", "L0_gnn_b_core", "L0_gnn_gamma_core", "L0_gnn_beta_core"]


def kernel(**inputs):
    import numpy as np
    import concourse.bacc as bacc
    from concourse.bass_utils import run_bass_kernel_spmd

    nc = bacc.Bacc("TRN2", target_bir_lowering=False, num_devices=1)
    arrays, args = {}, []
    for name in _INS:
        a = np.ascontiguousarray(inputs[name])
        arrays[f"in_{name}"] = a
        args.append(nc.dram_tensor(f"in_{name}", a.shape, mybir.dt.from_np(a.dtype), kind="ExternalInput").ap())
    out = nc.dram_tensor("out", arrays["in_x"].shape, F32, kind="ExternalOutput").ap()
    gnn_layer(nc, *args, out)
    r = run_bass_kernel_spmd(nc, [arrays], core_ids=[0])
    return r.results[0]["out"]
```
